# Optimizing a Trainium2 kernel written in Bass

```python
import numpy as np
import jax
import jax.numpy as jnp

def _softmax(x, axis=-1):
    return jax.nn.softmax(x, axis=axis)

def _gelu(x):
    return jax.nn.gelu(x, approximate=True)

def _silu(x):
    return jax.nn.silu(x)

def _sigmoid(x):
    return jax.nn.sigmoid(x)

def _layernorm(x, axis=-1, eps=1e-05):
    m = jnp.mean(x, axis=axis, keepdims=True)
    v = jnp.var(x, axis=axis, keepdims=True)
    return (x - m) / jnp.sqrt(v + eps)

def _scatter_add(tgt, idx, src, axis=0):
    return tgt.at[idx].add(src)

def _segment_sum(src, seg, n):
    return jax.ops.segment_sum(src, seg, n)
kernel_name = 'mk_adaln_ffn_d1_seqx_r4_6805c0'

def setup_inputs(seed: int=0):
    np.random.seed(seed)
    _w = jnp.asarray

    def _rec_inputs():
        import jax
        import jax.numpy as jnp
        _rk = jax.random.key(seed)
        x = -0.0003929 + 0.9999 * jax.random.normal(jax.random.fold_in(_rk, 1), (128, 64, 1024), jnp.float32)
        _lenS = 64 - jax.random.randint(jax.random.fold_in(_rk, 7), (128,), 0, max(1, 64 // 4) + 1, jnp.int32)
        _lenS2 = 64 - jax.random.randint(jax.random.fold_in(_rk, 8), (128,), 0, max(1, 64 // 4) + 1, jnp.int32)
        itok_B_78_3631 = jax.random.randint(jax.random.fold_in(_rk, 11), (128,), 78, 908, jnp.int32)
        return (x, itok_B_78_3631)
    x, itok_B_78_3631 = _rec_inputs()

    def _L0_cond_setup():
        import math
        import jax, jax.numpy as jnp
        import numpy as np
        B, H, N, L = (16, 64, 64, 1024)
        DT_MIN, DT_MAX = (0.001, 0.1)

        def _get_kernel(log_dt, C, log_A_real, A_imag, length):
            dt = jnp.exp(log_dt)
            Cc = C[..., 0] + 1j * C[..., 1]
            A = -jnp.exp(log_A_real) + 1j * A_imag
            dtA = A * dt[:, None]
            Ct = Cc * (jnp.exp(dtA) - 1.0) / A
            P = dtA[:, :, None] * jnp.arange(length, dtype=jnp.float32)
            K = 2.0 * jnp.einsum('hn,hnl->hl', Ct, jnp.exp(P)).real
            return K
        key = jax.random.key(seed)
        ks = jax.random.split(key, 5)
        u = jax.random.normal(ks[0], (B, H, L), dtype=jnp.float32)
        log_dt = jax.random.uniform(ks[1], (H,), dtype=jnp.float32) * (math.log(DT_MAX) - math.log(DT_MIN)) + math.log(DT_MIN)
        C = jax.random.normal(ks[2], (H, N, 2), dtype=jnp.float32)
        log_A_real = jnp.log(0.5 * jnp.ones((H, N), dtype=jnp.float32))
        A_imag = math.pi * jnp.broadcast_to(jnp.arange(N, dtype=jnp.float32), (H, N))
        D = jax.random.normal(ks[3], (H,), dtype=jnp.float32)
        length = jax.random.randint(ks[4], (B,), 1, L + 1, dtype=jnp.int32)
        return {'u': u, 'log_dt': log_dt, 'C': C, 'log_A_real': log_A_real, 'A_imag': A_imag, 'D': D, 'length': length}
    _L0_cond_all = _L0_cond_setup()
    _L0_cond_in = {k: v for k, v in _L0_cond_all.items() if k in ('log_dt', 'C', 'log_A_real', 'A_imag', 'D')}
    del _L0_cond_all

    def _L0_ffn_setup():
        import jax, jax.numpy as jnp
        import numpy as np
        K_TOP = 8
        key = jax.random.key(seed)
        k1, k2, k3 = jax.random.split(key, 3)
        B, S, H, E = (4, 1024, 1024, 64)
        hidden_states = jax.random.normal(k1, (B, S, H), dtype=jnp.float32)
        router_weight = jax.random.normal(k2, (E, H), dtype=jnp.float32)
        router_bias = jnp.zeros((E,), dtype=jnp.float32)
        expert_bias = jax.random.normal(k3, (E, H), dtype=jnp.float32) * 0.1
        return {'hidden_states': hidden_states, 'router_weight': router_weight, 'router_bias': router_bias, 'expert_bias': expert_bias}
    _L0_ffn_all = _L0_ffn_setup()
    _L0_ffn_in = {k: v for k, v in _L0_ffn_all.items() if k in ('router_weight', 'router_bias', 'expert_bias')}
    del _L0_ffn_all
    return {'x': x, 'itok_B_78_3631': itok_B_78_3631, 'L0_cond_log_dt': _L0_cond_in['log_dt'], 'L0_cond_C': _L0_cond_in['C'], 'L0_cond_log_A_real': _L0_cond_in['log_A_real'], 'L0_cond_A_imag': _L0_cond_in['A_imag'], 'L0_cond_D': _L0_cond_in['D'], 'L0_ffn_router_weight': _L0_ffn_in['router_weight'], 'L0_ffn_router_bias': _L0_ffn_in['router_bias'], 'L0_ffn_expert_bias': _L0_ffn_in['expert_bias']}

def reference(x, itok_B_78_3631, L0_cond_log_dt, L0_cond_C, L0_cond_log_A_real, L0_cond_A_imag, L0_cond_D, L0_ffn_router_weight, L0_ffn_router_bias, L0_ffn_expert_bias):
    import jax
    import jax.numpy as jnp

    def _L0_cond_ref(u, log_dt, C, log_A_real, A_imag, D, length):
        import math
        import jax, jax.numpy as jnp
        import numpy as np
        B, H, N, L = (16, 64, 64, 1024)
        DT_MIN, DT_MAX = (0.001, 0.1)

        def _get_kernel(log_dt, C, log_A_real, A_imag, length):
            dt = jnp.exp(log_dt)
            Cc = C[..., 0] + 1j * C[..., 1]
            A = -jnp.exp(log_A_real) + 1j * A_imag
            dtA = A * dt[:, None]
            Ct = Cc * (jnp.exp(dtA) - 1.0) / A
            P = dtA[:, :, None] * jnp.arange(length, dtype=jnp.float32)
            K = 2.0 * jnp.einsum('hn,hnl->hl', Ct, jnp.exp(P)).real
            return K
        Bq, Hq, Lq = u.shape
        K = _get_kernel(log_dt, C, log_A_real, A_imag, Lq)
        n = 2 * Lq
        kf = jnp.fft.rfft(K, n=n)
        uf = jnp.fft.rfft(u, n=n)
        y = jnp.fft.irfft(uf * kf[None], n=n)[..., :Lq]
        y = y + u * D[:, None]
        mask = (jnp.arange(Lq)[None, :] < length[:, None]).astype(u.dtype)
        return y * mask[:, None, :]

    def _L0_ffn_ref(hidden_states, router_weight, router_bias, expert_bias):
        import jax, jax.numpy as jnp
        import numpy as np
        K_TOP = 8
        B, S, H = hidden_states.shape
        E = router_weight.shape[0]
        T = B * S
        flat = hidden_states.reshape(T, H)
        logits = jnp.einsum('th,eh->te', flat, router_weight) + router_bias
        scores = jax.nn.softmax(logits, axis=-1)
        topk_w, topk_idx = jax.lax.top_k(scores, K_TOP)
        w_sum = topk_w.sum(axis=-1, keepdims=True)
        w_dense = jnp.zeros((T, E), dtype=scores.dtype).at[jnp.arange(T)[:, None], topk_idx].add(topk_w)
        bias_mix = jnp.einsum('te,eh->th', w_dense, expert_bias)
        out = flat * w_sum + bias_mix
        return out.reshape(B, S, H)
    x = x + _L0_ffn_ref(_L0_cond_ref(x, L0_cond_log_dt, L0_cond_C, L0_cond_log_A_real, L0_cond_A_imag, L0_cond_D, itok_B_78_3631), L0_ffn_router_weight, L0_ffn_router_bias, L0_ffn_expert_bias)
    return x

_drawn_inputs = setup_inputs


def setup_inputs(seed=0):
    import zlib

    import numpy as np

    out = dict(_drawn_inputs(seed))
    spreads = {'L0_cond_log_A_real': (-0.6931471824645996, 0.2), 'L0_ffn_router_bias': (0.0, 0.1)}
    factors = {}
    for name, (base, spread) in spreads.items():
        noise = np.random.default_rng([zlib.crc32(name.encode()), seed]).standard_normal(out[name].shape)
        drawn = base * np.exp(spread * noise) if base else spread * noise
        out[name] = jnp.asarray(drawn.astype(out[name].dtype))
    for name, factor in factors.items():
        out[name] = (out[name] * factor).astype(out[name].dtype)
    return out
```

```python
from contextlib import ExitStack

import numpy as np

import concourse.bass as bass
from concourse import mybir

F32 = mybir.dt.float32
F32R = mybir.dt.float32r
I32 = mybir.dt.int32
ALU = mybir.AluOpType
ACT = mybir.ActivationFunctionType

P = 128
B, H, L = 128, 64, 1024
N, E, TOP = 64, 64, 8
NC = L // P
HALF = NC // 2
G = H // 2
UNROLL = 4
HB = 2 * UNROLL
NI, NA = 64, L // 64
NJ = NI + 2 * NA
ROW = P + L

ROUND = 1.5 * 2.0 ** 23
ROUND18 = 1.5 * 2.0 ** 5
TWO_PI = 6.283184
LOWEST = -3.4028235e38
LN2_HI, LN2_LO = 0.693359375, -2.12194440e-4
LOG2_E = 1.4426950408889634


def inverse_two_pi_parts():
    x = 1.0 / (2.0 * np.pi)
    c1 = np.round(x * 2 ** 14) / 2 ** 14
    c2 = np.round((x - c1) * 2 ** 26) / 2 ** 26
    return float(c1), float(c2), float(x - c1 - c2)


def build(nc, x, x_rev, lens, modes, d_skip, router, router_bias, expert_bias, steps, offsets, l_index,
          identity, fold, out):
    ctx = ExitStack()
    with ctx:
        def sb(name, shape, dt=F32):
            return ctx.enter_context(nc.sbuf_tensor(name, shape, dt))

        def ps(name, shape):
            return ctx.enter_context(nc.psum_tensor(name, shape, F32))

        def sem(name):
            return ctx.enter_context(nc.semaphore(name))

        filters = nc.dram_tensor("filters", [H, ROW], F32, kind="Internal").ap()
        toeplitz = bass.AP(filters.tensor, filters.offset + 1, [[ROW, H], [1, P], [1, L]])

        xs = [sb(f"xs{i}", [P, NC, 2, B]) for i in range(2)]
        us = [sb(f"us{i}", [P, NC, 2, B]) for i in range(2)]
        u_hi = [sb(f"u_hi{i}", [P, NC, 2, B], F32R) for i in range(2)]
        u_lo = [sb(f"u_lo{i}", [P, NC, 2, B], F32R) for i in range(2)]
        toe = [sb(f"toe{i}", [P, L]) for i in range(4)]
        toe_hi = [sb(f"toe_hi{i}", [P, L], F32R) for i in range(2)]
        toe_lo = [sb(f"toe_lo{i}", [P, L], F32R) for i in range(2)]
        zs = [sb(f"zs{i}", [P, NC, 2, B]) for i in range(4)]
        mask = sb("mask", [P, NC, B])
        len_i = sb("len_i", [P, B], I32)
        len_f = sb("len_f", [P, B])
        l_idx = sb("l_idx", [P, NC])
        rwt = sb("rwt", [P, NC, E])
        rbias = sb("rbias", [P, 1])
        ebt = sb("ebt", [P, L])
        ebt_hi = sb("ebt_hi", [P, L], F32R)
        ebt_lo = sb("ebt_lo", [P, L], F32R)
        ident = sb("ident", [P, P])
        fold_sb = sb("fold_sb", [P, E])
        ones = sb("ones", [P, P], F32R)
        logit_t = sb("logit_t", [P, 2 * B])
        token = sb("token", [P, 2, E])
        top8 = sb("top8", [P, 2, TOP])
        neg_max = sb("neg_max", [P, 2])
        escore = sb("escore", [P, 2, E])
        esum = sb("esum", [P, 2])
        rsum = sb("rsum", [P, 2])
        dropped = sb("dropped", [P, 2, E])
        kept = sb("kept", [P, 2, E])
        weight2 = sb("weight2", [P, 2, 2, E])
        weight_t = sb("weight_t", [P, 2 * B], F32R)
        md = sb("md", [P, 5, H])
        dsk = sb("dsk", [1, H])
        st = sb("st", [P, NJ])
        off = sb("off", [P, NJ])
        cx = sb("cx", [P, 26, H])
        cb_hi = sb("cb_hi", [P, H], F32R)
        ci = sb("ci", [P, 2, H], I32)
        turn_hi = sb("turn_hi", [P, H])
        turn_lo = sb("turn_lo", [P, H])
        decay = sb("decay", [P, H])
        coef_own = sb("coef_own", [P, H])
        coef_oth = sb("coef_oth", [P, H])
        ph = sb("ph", [P, HB, NJ])
        ph_int = sb("ph_int", [P, HB, NJ])
        ph_lo = sb("ph_lo", [P, HB, NJ])
        dec = sb("dec", [P, HB, NI + NA])
        sn = sb("sn", [P, HB, NJ])
        ex = sb("ex", [P, HB, NI + NA])
        w_own = sb("w_own", [P, HB, NA])
        w_oth = sb("w_oth", [P, HB, NA])
        tab_v = sb("tab_v", [P, HB, NI])
        tab_w = sb("tab_w", [P, HB, NA])
        k_sb = sb("k_sb", [NA, 2, NI])
        zeros = sb("zeros", [H, P])

        y = [ps(f"y{i}", [P, NC, B]) for i in range(2)]
        bank_t = ps("bank_t", [P, 512])
        bank_s = ps("bank_s", [P, 512])
        bias_p = ps("bias_p", [P, 2, 2, 2 * B])
        logit_p = bank_t[:, 0:256]
        weight_p = bank_t[:, 256:512]
        token_p = bank_s[:, 0:128]
        wsum_p = bank_s[:, 128:384]
        filter_p = bank_s[0:NA, 384:512]

        x_loaded = [sem(f"x_loaded{i}") for i in range(2)]
        u_loaded = [sem(f"u_loaded{i}") for i in range(2)]
        toe_loaded = [sem(f"toe_loaded{i}") for i in range(4)]
        out_stored = [sem(f"out_stored{i}") for i in range(4)]
        modes_loaded = sem("modes_loaded")
        consts_loaded = sem("consts_loaded")
        zeros_made = sem("zeros_made")
        pad_written = sem("pad_written")
        filter_written = sem("filter_written")
        const_step = sem("const_step")
        const_hi = sem("const_hi")
        mask_ready = sem("mask_ready")
        tab_pool = sem("tab_pool")
        tab_dve = sem("tab_dve")
        tab_act = sem("tab_act")
        filter_mm = sem("filter_mm")
        k_copied = sem("k_copied")
        k_full = sem("k_full")
        toe_hi_ready = sem("toe_hi_ready")
        toe_lo_ready = sem("toe_lo_ready")
        u_hi_ready = sem("u_hi_ready")
        u_lo_ready = sem("u_lo_ready")
        conv_half = sem("conv_half")
        z_half = sem("z_half")
        logits_mm = sem("logits_mm")
        logit_t_ready = sem("logit_t_ready")
        token_mm = sem("token_mm")
        token_ready = sem("token_ready")
        max_step = sem("max_step")
        exp_done = sem("exp_done")
        drop_done = sem("drop_done")
        kept_step = sem("kept_step")
        weights_ready = sem("weights_ready")
        weight_mm = sem("weight_mm")
        weight_hi_ready = sem("weight_hi_ready")
        weight_t_ready = sem("weight_t_ready")
        expert_hi_ready = sem("expert_hi_ready")
        expert_lo_ready = sem("expert_lo_ready")
        wsum_mm = sem("wsum_mm")
        bias_mm = sem("bias_mm")
        scaled = sem("scaled")
        mixed = sem("mixed")
        final = sem("final")

        block = ctx.enter_context(nc.Block())

        def run(eng, group, last):
            for g in range(UNROLL):
                group(g, 0, g)
            with eng.Fori(1, G // UNROLL - 1, 1) as it:
                for k in range(UNROLL):
                    group(it * UNROLL + k, it, k)
            for g in range(G - UNROLL, last):
                group(g, g // UNROLL, g % UNROLL)

        def there(g):
            return 0 <= g < G if isinstance(g, int) else True

        @block.sync
        def _(sp):
            sp.dma_start(md[:, :, :], modes).then_inc(modes_loaded, 16)
            sp.dma_start(st[:, :], steps).then_inc(modes_loaded, 16)
            sp.dma_start(off[:, :], offsets).then_inc(modes_loaded, 16)
            sp.dma_start(dsk[:, :], d_skip).then_inc(modes_loaded, 16)
            sp.dma_start(us[0][:, :, :, :], x_rev[0]).then_inc(u_loaded[0], 16)
            sp.dma_start(len_i[:, :], lens).then_inc(consts_loaded, 16)
            sp.dma_start(l_idx[:, :], l_index).then_inc(consts_loaded, 16)
            sp.dma_start(rwt[:, :, :], router).then_inc(consts_loaded, 16)
            sp.dma_start(rbias[:, :], router_bias).then_inc(consts_loaded, 16)
            sp.dma_start(ebt[:, :], expert_bias).then_inc(consts_loaded, 16)
            sp.dma_start(ident[:, :], identity).then_inc(consts_loaded, 16)
            sp.dma_start(fold_sb[:, :], fold).then_inc(consts_loaded, 16)
            sp.dma_start(us[1][:, :, :, :], x_rev[1]).then_inc(u_loaded[1], 16)
            sp.wait_ge(zeros_made, 1)
            sp.dma_start(filters[:, 0:P], zeros[:, :]).then_inc(pad_written, 16)

            def write_filter(g):
                sp.wait_ge(k_full, g + 1)
                sp.dma_start(filters[bass.ts(g, 2), P:ROW].rearrange("s (a i) -> a s i", a=NA), k_sb[:, :, :])\
                  .then_inc(filter_written, 16)

            def load_toeplitz(g, k):
                for j in range(2):
                    slot = (2 * k + j) % 4
                    if not (isinstance(g, int) and g < 2):
                        sp.wait_ge(toe_lo_ready, 2 * g + j - 3)
                    if j == 0:
                        sp.wait_ge(filter_written, 16 * g + 16)
                    sp.dma_start(toe[slot][:, :], toeplitz[2 * g + j]).then_inc(toe_loaded[slot], 16)

            sp.wait_ge(pad_written, 16)
            write_filter(0)
            load_toeplitz(0, 0)
            write_filter(1)

            def group(g, it, k):
                if there(g + 2):
                    sp.wait_ge(u_lo_ready, g + 1)
                    sp.dma_start(us[k % 2][:, :, :, :], x_rev[g + 2]).then_inc(u_loaded[k % 2], 16)
                if there(g + 1):
                    load_toeplitz(g + 1, k + 1)
                if there(g - 2):
                    for half in range(2):
                        sp.wait_ge(final, 2 * g - 3 + half)
                        cs = slice(half * HALF, (half + 1) * HALF)
                        sp.dma_start(out[g - 2].rearrange("p (c n) -> p c n", c=NC)[:, cs, :],
                                     zs[(k - 2) % 4][:, cs, :, :].rearrange("p c j b -> p c (j b)"))\
                          .then_inc(out_stored[(k - 2) % 4], 16)
                if there(g):
                    sp.dma_start(xs[k % 2][:, :, :, :], x[g]).then_inc(x_loaded[k % 2], 16)
                if there(g + 2):
                    write_filter(g + 2)

            run(sp, group, G + 2)
            for i in range(4):
                sp.wait_ge(out_stored[i], 32 * (G // 4))

        @block.gpsimd
        def _(pool):
            nc.gpsimd.memset(zeros[:, :], 0.0).then_inc(zeros_made, 1)
            nc.gpsimd.memset(ones[:, :].bitcast(F32), 1.0).then_inc(zeros_made, 1)

            def tables(nb):
                hs = bass.ts(nb, HB)
                stb = st[:, :].unsqueeze(1).broadcast_to([P, HB, NJ])
                offb = off[:, :].unsqueeze(1).broadcast_to([P, HB, NJ])
                if not (isinstance(nb, int) and nb == 0):
                    pool.wait_ge(tab_dve, 10 * nb)
                pool.wait_ge(modes_loaded, 64)
                nc.gpsimd.tensor_tensor(ph[:, :, :], turn_hi[:, hs].unsqueeze(2).broadcast_to([P, HB, NJ]), stb,
                                        ALU.mult).then_inc(tab_pool, 1)
                pool.wait_ge(tab_pool, 4 * nb + 1)
                nc.gpsimd.tensor_tensor(ph[:, :, :], ph[:, :, :], offb, ALU.add).then_inc(tab_pool, 1)
                nc.gpsimd.tensor_tensor(ph_lo[:, :, :], turn_lo[:, hs].unsqueeze(2).broadcast_to([P, HB, NJ]), stb,
                                        ALU.mult).then_inc(tab_pool, 1)
                nc.gpsimd.tensor_tensor(dec[:, :, :],
                                        decay[:, hs].unsqueeze(2).broadcast_to([P, HB, NI + NA]),
                                        st[:, 0:NI + NA].unsqueeze(1).broadcast_to([P, HB, NI + NA]),
                                        ALU.mult).then_inc(tab_pool, 1)

            def residual(g, it, k, half):
                cs = slice(half * HALF, (half + 1) * HALF)
                pool.wait_ge(x_loaded[k % 2], 32 * it + 16 * (k // 2) + 16)
                pool.wait_ge(mixed, 2 * g + half + 1)
                nc.gpsimd.tensor_tensor(zs[k % 4][:, cs, :, :], zs[k % 4][:, cs, :, :], xs[k % 2][:, cs, :, :],
                                        ALU.add).then_inc(final, 1)

            def split_toeplitz(g, k, j):
                pool.wait_ge(toe_hi_ready, 2 * g + j + 1)
                nc.gpsimd.tensor_tensor(toe_lo[j][:, :], toe[(2 * k + j) % 4][:, :], toe_hi[j][:, :].bitcast(F32),
                                        ALU.subtract).then_inc(toe_lo_ready, 1)

            pool.wait_ge(const_step, 1000)
            tables(0)
            split_toeplitz(0, 0, 0)

            def group(g, it, k):
                if there(g):
                    split_toeplitz(g, k, 1)
                if there(g - 2):
                    residual(g - 2, it, k - 2, 0)
                if there(g + 1):
                    split_toeplitz(g + 1, k + 1, 0)
                if there(g - 2):
                    residual(g - 2, it, k - 2, 1)
                if k == 0 and there(g + UNROLL):
                    tables(it + 1)

            run(pool, group, G + 2)

        @block.scalar
        def _(act):
            def split(g, it, k):
                act.wait_ge(u_loaded[k % 2], 32 * it + 16 * (k // 2) + 16)
                if not (isinstance(g, int) and g < 2):
                    act.wait_ge(conv_half, 4 * g - 4)
                nc.scalar.activation(u_hi[k % 2][:, :, :, :], us[k % 2][:, :, :, :], ACT.Copy)\
                  .then_inc(u_hi_ready, 1)

            def tables(nb):
                act.wait_ge(tab_dve, 10 * nb + 5)
                nc.scalar.activation(sn[:, :, :], ph[:, :, :], ACT.Sin, scale=TWO_PI).then_inc(tab_act, 1)
                act.wait_ge(tab_pool, 4 * nb + 4)
                nc.scalar.activation(ex[:, :, :], dec[:, :, :], ACT.Exp).then_inc(tab_act, 1)

            def take_filter(g):
                if not (isinstance(g, int) and g == 0):
                    act.wait_ge(filter_written, 16 * g)
                act.wait_ge(filter_mm, g + 1)
                nc.scalar.activation(k_sb[:, :, :].rearrange("a j i -> a (j i)"), filter_p, ACT.Copy)\
                  .then_inc(k_copied, 1)

            def split_toeplitz(g, it, k, j):
                slot = (2 * k + j) % 4
                act.wait_ge(toe_loaded[slot], 32 * it + 16 * ((2 * k + j) // 4) + 16)
                if not (isinstance(g, int) and g == 0):
                    act.wait_ge(conv_half, 4 * g + 2 * j - 2)
                nc.scalar.activation(toe_hi[j][:, :], toe[slot][:, :], ACT.Copy).then_inc(toe_hi_ready, 1)

            act.wait_ge(const_hi, 1)
            nc.scalar.activation(cb_hi[:, :], cx[:, 0, :], ACT.Copy).then_inc(const_hi, 1)
            act.wait_ge(const_hi, 3)
            nc.scalar.activation(cx[:, 10, :], cx[:, 9, :], ACT.Sin, scale=TWO_PI).then_inc(const_hi, 1)
            nc.scalar.activation(cx[:, 11, :], cx[:, 9, :], ACT.Sin, scale=TWO_PI / 2).then_inc(const_hi, 1)
            split(0, 0, 0)
            tables(0)
            take_filter(0)
            take_filter(1)
            split_toeplitz(0, 0, 0, 0)
            act.wait_ge(consts_loaded, 112)
            nc.scalar.activation(ebt_hi[:, :], ebt[:, :], ACT.Copy).then_inc(expert_hi_ready, 1)

            def group(g, it, k):
                if there(g - 2):
                    act.wait_ge(weight_mm, g - 1)
                    if not (isinstance(g, int) and g == 2):
                        act.wait_ge(bias_mm, 2 * (g - 2))
                    nc.scalar.activation(weight_t[:, :], weight_p, ACT.Copy).then_inc(weight_hi_ready, 1)
                if there(g):
                    split_toeplitz(g, it, k, 1)
                if there(g + 1):
                    split(g + 1, it, k + 1)
                if there(g - 1):
                    act.wait_ge(logits_mm, g)
                    nc.scalar.activation(logit_t[:, :], logit_p, ACT.Identity, bias=rbias[:, 0:1])\
                      .then_inc(logit_t_ready, 1)
                if there(g - 1):
                    act.wait_ge(token_mm, g)
                    if not (isinstance(g, int) and g == 1):
                        act.wait_ge(weights_ready, g - 1)
                    nc.scalar.activation(token[:, :, :].rearrange("p j e -> p (j e)"), token_p, ACT.Copy)\
                      .then_inc(token_ready, 1)
                if there(g + 2):
                    take_filter(g + 2)
                if there(g + 1):
                    split_toeplitz(g + 1, it, k + 1, 0)
                if there(g - 1):
                    act.wait_ge(max_step, 3 * g)
                    for j in range(2):
                        ins = nc.scalar.activation(escore[:, j, :], token[:, j, :], ACT.Exp,
                                                   bias=neg_max[:, j:j + 1], accum_out=esum[:, j:j + 1])
                    ins.then_inc(exp_done, 1)
                if k == 1 and there(g + UNROLL - 1):
                    tables(it + 1)

            run(act, group, G + 2)

        @block.vector
        def _(dve):
            steps_done = [0]

            def link(ins):
                steps_done[0] += 1
                ins.then_inc(const_step, 1)
                dve.wait_ge(const_step, steps_done[0])

            def tt(o, a, b, op):
                link(nc.vector.tensor_tensor(o, a, b, op))

            def ts(o, a, s1, s2, op0, op1):
                link(nc.vector.tensor_scalar(o, a, s1, s2, op0, op1))

            def stt(o, a, s, b, op0, op1):
                link(nc.vector.scalar_tensor_tensor(o, a, s, b, op0, op1))

            def exp_parts(xin, k, r, q, scale_int):
                ts(k, xin, LOG2_E, ROUND, ALU.mult, ALU.add)
                ts(k, k, ROUND, None, ALU.subtract, ALU.bypass)
                ts(k, k, -126.0, 127.0, ALU.max, ALU.min)
                stt(r, k, -LN2_HI, xin, ALU.mult, ALU.add)
                stt(r, k, -LN2_LO, r, ALU.mult, ALU.add)
                ts(scale_int, k, 127.0, 2.0 ** 23, ALU.add, ALU.mult)
                ts(q, r, 1.0 / 5040, None, ALU.mult, ALU.bypass)
                for c in (1.0 / 720, 1.0 / 120, 1.0 / 24, 1.0 / 6, 0.5, 1.0):
                    stt(q, q, c, r, ALU.add, ALU.mult)

            c = [cx[:, i, :] for i in range(26)]
            dve.wait_ge(modes_loaded, 64)
            pair = cx[:, 12:14, :]
            exp_parts(md[:, 0:2, :], cx[:, 14:16, :], cx[:, 16:18, :], cx[:, 18:20, :], ci[:, :, :])
            stt(pair, cx[:, 18:20, :], 1.0, ci[:, :, :].bitcast(F32), ALU.add, ALU.mult)
            dt, are, aim = cx[:, 12, :], cx[:, 13, :], md[:, 2, :]
            tt(c[0], aim, dt, ALU.mult)
            stt(decay[:, :], are, -1.0, dt, ALU.mult, ALU.mult)
            dve.sem_inc(const_hi, 1)
            c1, c2, c3 = inverse_two_pi_parts()
            dve.wait_ge(const_hi, 2)
            bh = cb_hi[:, :].bitcast(F32)
            tt(c[1], c[0], bh, ALU.subtract)
            ts(c[2], bh, c1, None, ALU.mult, ALU.bypass)
            ts(c[3], c[2], ROUND, ROUND, ALU.add, ALU.subtract)
            tt(c[2], c[2], c[3], ALU.subtract)
            ts(c[4], c[1], c1, None, ALU.mult, ALU.bypass)
            ts(c[5], bh, c2, None, ALU.mult, ALU.bypass)
            tt(c[3], c[2], c[4], ALU.add)
            tt(c[3], c[3], c[5], ALU.add)
            ts(turn_hi[:, :], c[3], ROUND18, ROUND18, ALU.add, ALU.subtract)
            tt(c[2], c[2], turn_hi[:, :], ALU.subtract)
            tt(c[2], c[2], c[4], ALU.add)
            tt(c[2], c[2], c[5], ALU.add)
            stt(c[2], bh, c3, c[2], ALU.mult, ALU.add)
            stt(turn_lo[:, :], c[1], c2, c[2], ALU.mult, ALU.add)
            tt(c[8], turn_hi[:, :], turn_lo[:, :], ALU.add)
            ts(c[7], c[8], ROUND, ROUND, ALU.add, ALU.subtract)
            tt(c[9], c[8], c[7], ALU.subtract)
            dve.sem_inc(const_hi, 1)
            exp_parts(decay[:, :], c[14], c[15], c[16], ci[:, 0, :])
            two_k = ci[:, 0, :].bitcast(F32)
            stt(c[17], c[16], 1.0, two_k, ALU.add, ALU.mult)
            tt(c[18], c[16], two_k, ALU.mult)
            stt(c[18], two_k, -1.0, c[18], ALU.add, ALU.add)
            dve.wait_ge(const_hi, 5)
            stt(c[19], c[11], -2.0, c[11], ALU.mult, ALU.mult)
            tt(c[20], c[19], c[17], ALU.mult)
            tt(c[20], c[20], c[18], ALU.add)
            tt(c[21], c[17], c[10], ALU.mult)
            tt(c[1], md[:, 3, :], c[20], ALU.mult)
            tt(c[2], md[:, 4, :], c[21], ALU.mult)
            tt(c[1], c[1], c[2], ALU.subtract)
            tt(c[2], md[:, 3, :], c[21], ALU.mult)
            tt(c[3], md[:, 4, :], c[20], ALU.mult)
            tt(c[2], c[2], c[3], ALU.add)
            tt(c[4], are, are, ALU.mult)
            tt(c[5], aim, aim, ALU.mult)
            tt(c[4], c[4], c[5], ALU.add)
            link(nc.vector.reciprocal(c[4], c[4]))
            tt(c[5], c[2], aim, ALU.mult)
            tt(c[6], c[1], are, ALU.mult)
            tt(c[5], c[5], c[6], ALU.subtract)
            tt(c[22], c[5], c[4], ALU.mult)
            tt(c[5], c[2], are, ALU.mult)
            tt(c[6], c[1], aim, ALU.mult)
            tt(c[5], c[5], c[6], ALU.add)
            tt(c[23], c[5], c[4], ALU.mult)
            ts(coef_own[0:N, :], cx[0:N, 22, :], 2.0, None, ALU.mult, ALU.bypass)
            ts(coef_own[N:P, :], cx[N:P, 22, :], -2.0, None, ALU.mult, ALU.bypass)
            ts(coef_oth[:, :], c[23], 2.0, None, ALU.mult, ALU.bypass)
            dve.sem_inc(const_step, 1000 - steps_done[0])

            def tables(nb, part):
                hs = bass.ts(nb, HB)
                def done(n):
                    dve.wait_ge(tab_dve, 10 * nb + n)
                if part == 0:
                    dve.wait_ge(tab_pool, 4 * nb + 3)
                    nc.vector.tensor_scalar(ph_int[:, :, :], ph[:, :, :], ROUND, ROUND, ALU.add, ALU.subtract)\
                      .then_inc(tab_dve, 1)
                    done(1)
                    nc.vector.tensor_tensor(ph[:, :, :], ph[:, :, :], ph_int[:, :, :], ALU.subtract)\
                      .then_inc(tab_dve, 1)
                    done(2)
                    nc.vector.tensor_tensor(ph[:, :, :], ph[:, :, :], ph_lo[:, :, :], ALU.add)\
                      .then_inc(tab_dve, 1)
                    done(3)
                    nc.vector.tensor_scalar(ph_int[:, :, :], ph[:, :, :], ROUND, ROUND, ALU.add, ALU.subtract)\
                      .then_inc(tab_dve, 1)
                    done(4)
                    nc.vector.tensor_tensor(ph[:, :, :], ph[:, :, :], ph_int[:, :, :], ALU.subtract)\
                      .then_inc(tab_dve, 1)
                else:
                    dve.wait_ge(tab_act, 2 * nb + 2)
                    if not (isinstance(nb, int) and nb == 0):
                        dve.wait_ge(filter_mm, UNROLL * nb)
                    nc.vector.tensor_tensor(tab_v[:, :, :], sn[:, :, 0:NI], ex[:, :, 0:NI], ALU.mult)\
                      .then_inc(tab_dve, 1)
                    nc.vector.tensor_tensor(w_own[:, :, :], sn[:, :, NI:NI + NA],
                                            coef_own[:, hs].unsqueeze(2).broadcast_to([P, HB, NA]), ALU.mult)\
                      .then_inc(tab_dve, 1)
                    nc.vector.tensor_tensor(w_oth[:, :, :], sn[:, :, NI + NA:NJ],
                                            coef_oth[:, hs].unsqueeze(2).broadcast_to([P, HB, NA]), ALU.mult)\
                      .then_inc(tab_dve, 1)
                    done(8)
                    nc.vector.tensor_tensor(w_own[:, :, :], w_own[:, :, :], w_oth[:, :, :], ALU.add)\
                      .then_inc(tab_dve, 1)
                    done(9)
                    nc.vector.tensor_tensor(tab_w[:, :, :], w_own[:, :, :], ex[:, :, NI:NI + NA], ALU.mult)\
                      .then_inc(tab_dve, 1)

            def add_skip(g):
                dve.wait_ge(k_copied, g + 1)
                nc.vector.tensor_tensor(k_sb[0:1, :, 0], k_sb[0:1, :, 0], dsk[0:1, bass.ts(g, 2)], ALU.add)\
                  .then_inc(k_full, 1)

            def split(g, k):
                dve.wait_ge(u_hi_ready, g + 1)
                nc.vector.tensor_tensor(u_lo[k % 2][:, :, :, :], us[k % 2][:, :, :, :],
                                        u_hi[k % 2][:, :, :, :].bitcast(F32), ALU.subtract)\
                  .then_inc(u_lo_ready, 1)

            def masked(g, it, k, j, half):
                cs = slice(half * HALF, (half + 1) * HALF)
                if j == 0 and half == 0 and not (isinstance(g, int) and g < 4):
                    dve.wait_ge(out_stored[k], 32 * it)
                dve.wait_ge(conv_half, 4 * g + 2 * j + half + 1)
                nc.vector.tensor_tensor(zs[k][:, cs, j, :], y[j][:, cs, :], mask[:, cs, :], ALU.mult)\
                  .then_inc(z_half, 1)

            def softmax(g):
                dve.wait_ge(token_ready, g + 1)
                if there(g + 3):
                    add_skip(g + 3)
                for j in range(2):
                    nc.vector.max(top8[:, j, :], token[:, j, :]).then_inc(max_step, 1)
                dve.wait_ge(max_step, 3 * g + 2)
                nc.vector.tensor_scalar(neg_max[:, :], top8[:, :, 0], -1.0, None, ALU.mult, ALU.bypass)\
                  .then_inc(max_step, 1)
                for j in range(2):
                    ins = nc.vector.match_replace(out=dropped[:, j, :], in_to_replace=top8[:, j, :],
                                                  in_values=token[:, j, :], imm_value=LOWEST)
                ins.then_inc(drop_done, 1)
                dve.wait_ge(exp_done, g + 1)
                nc.vector.reciprocal(rsum[:, :], esum[:, :]).then_inc(kept_step, 1)
                dve.wait_ge(drop_done, g + 1)
                nc.vector.scalar_tensor_tensor(kept[:, :, :], dropped[:, :, :], LOWEST, escore[:, :, :],
                                               ALU.is_equal, ALU.mult).then_inc(kept_step, 1)
                dve.wait_ge(kept_step, 2 * g + 2)
                if not (isinstance(g, int) and g == 0):
                    dve.wait_ge(weight_mm, g)
                nc.vector.tensor_tensor(weight2[:, :, :, :], kept[:, :, :].unsqueeze(2).broadcast_to([P, 2, 2, E]),
                                        rsum[:, :].unsqueeze(2).unsqueeze(3).broadcast_to([P, 2, 2, E]), ALU.mult)\
                  .then_inc(weights_ready, 1)

            def low_weights(g):
                dve.wait_ge(weight_hi_ready, g + 1)
                nc.vector.tensor_tensor(weight_t[E:P, :], weight_p[E:P, :], weight_t[E:P, :].bitcast(F32),
                                        ALU.subtract).then_inc(weight_t_ready, 1)

            def scale(g, k):
                dve.wait_ge(wsum_mm, g + 1)
                nc.vector.tensor_tensor(zs[k % 4][:, :, :, :].rearrange("p c j b -> p c (j b)"),
                                        zs[k % 4][:, :, :, :].rearrange("p c j b -> p c (j b)"),
                                        wsum_p.unsqueeze(1).broadcast_to([P, NC, 2 * B]), ALU.mult)\
                  .then_inc(scaled, 1)

            def mix(g, k, half):
                cs = slice(half * HALF, (half + 1) * HALF)
                dve.wait_ge(bias_mm, 2 * g + half + 1)
                if half == 0:
                    dve.wait_ge(scaled, g + 1)
                zv = zs[k % 4][:, cs, :, :].rearrange("p (q t) j b -> p q t (j b)", t=2)
                nc.vector.tensor_tensor(zv, zv, bias_p[:, :, :, :].rearrange("p t q n -> p q t n"), ALU.add)\
                  .then_inc(mixed, 1)

            dve.wait_ge(consts_loaded, 112)
            nc.vector.tensor_copy(len_f[:, :], len_i[:, :]).then_inc(mask_ready, 1)
            dve.wait_ge(mask_ready, 1)
            for cc in range(NC):
                nc.vector.tensor_scalar(mask[:, cc, :], len_f[:, :], l_idx[:, cc:cc + 1], None, ALU.is_gt,
                                        ALU.bypass).then_inc(mask_ready, 1)
            dve.wait_ge(mask_ready, 1 + NC)
            tables(0, 0)
            tables(0, 1)
            split(0, 0)
            add_skip(0)
            add_skip(1)

            dve.wait_ge(expert_hi_ready, 1)
            nc.vector.tensor_tensor(ebt_lo[:, :], ebt[:, :], ebt_hi[:, :].bitcast(F32), ALU.subtract)\
              .then_inc(expert_lo_ready, 1)

            def group(g, it, k):
                if there(g - 2):
                    low_weights(g - 2)
                if there(g):
                    masked(g, it, k, 0, 0)
                if there(g - 2):
                    scale(g - 2, k - 2)
                    mix(g - 2, k - 2, 0)
                if there(g):
                    masked(g, it, k, 0, 1)
                if there(g - 2):
                    mix(g - 2, k - 2, 1)
                if there(g + 1):
                    split(g + 1, k + 1)
                if there(g + UNROLL - k):
                    if k == 1:
                        tables(it + 1, 0)
                    if k == 2:
                        tables(it + 1, 1)
                if there(g):
                    masked(g, it, k, 1, 0)
                if there(g - 1):
                    softmax(g - 1)
                elif there(g + 2):
                    add_skip(g + 2)
                if there(g):
                    masked(g, it, k, 1, 1)

            run(dve, group, G + 2)

        @block.tensor
        def _(pe):
            def filters_of(g, it, k):
                pe.wait_ge(tab_dve, 10 * (it + k // UNROLL) + 10)
                if not (isinstance(g, int) and g == 0):
                    pe.wait_ge(k_copied, g)
                for j in range(2):
                    hb = 2 * (k % UNROLL) + j
                    ins = nc.tensor.matmul(filter_p[:, j * NI:(j + 1) * NI], tab_w[:, hb, :], tab_v[:, hb, :],
                                           start=True, stop=True)
                ins.then_inc(filter_mm, 1)

            def convolve(g, it, k, j, half):
                first = HALF * half
                if half == 0:
                    pe.wait_ge(toe_lo_ready, 2 * g + j + 1)
                    if j == 0:
                        pe.wait_ge(u_lo_ready, g + 1)
                if not (isinstance(g, int) and g == 0):
                    pe.wait_ge(z_half, 4 * g + 2 * j + half - 3)
                parts = ((toe_hi[j], u_hi[k % 2]), (toe_hi[j], u_lo[k % 2]), (toe_lo[j], u_hi[k % 2]))
                work = [(0, 0)] + [(d, p) for d in range(1, first + HALF) for p in range(3)] + [(0, 1), (0, 2)]
                for n, (d, p) in enumerate(work):
                    tile, u = parts[p]
                    lo, hi = max(first, d), first + HALF
                    ins = nc.tensor.matmul(y[j][:, lo:hi, :], tile[:, d * P:(d + 1) * P],
                                           u[:, lo - d:hi - d, j, :], start=(n == 0), stop=(n == len(work) - 1))
                ins.then_inc(conv_half, 1)

            def logits(g, k):
                pe.wait_ge(z_half, 4 * g + 4)
                if not (isinstance(g, int) and g == 0):
                    pe.wait_ge(logit_t_ready, g)
                for q in range(NC // 2):
                    for odd in range(2):
                        ins = nc.tensor.matmul(logit_p[odd * E:(odd + 1) * E, :], rwt[:, 2 * q + odd, :],
                                               zs[k % 4][:, 2 * q + odd, :, :], start=(q == 0),
                                               stop=(q == NC // 2 - 1))
                ins.then_inc(logits_mm, 1)

            def tokens(g):
                pe.wait_ge(logit_t_ready, g + 1)
                pe.wait_ge(k_copied, min(g + 3, G) if isinstance(g, int) else g + 3)
                if not (isinstance(g, int) and g == 0):
                    pe.wait_ge(token_ready, g)
                for j in range(2):
                    ins = nc.tensor.matmul(token_p[:, j * E:(j + 1) * E], logit_t[:, j * B:(j + 1) * B],
                                           fold_sb[:, :], start=True, stop=True)
                ins.then_inc(token_mm, 1)

            def weights(g):
                pe.wait_ge(weights_ready, g + 1)
                if not (isinstance(g, int) and g == 0):
                    pe.wait_ge(weight_t_ready, g)
                for j in range(2):
                    ins = nc.tensor.transpose(weight_p[:, j * B:(j + 1) * B],
                                              weight2[:, j, :, :].rearrange("p t e -> p (t e)"), ident[:, :])
                ins.then_inc(weight_mm, 1)

            def bias(g, half):
                if half == 0:
                    pe.wait_ge(token_ready, g + 1)
                    pe.wait_ge(k_copied, min(g + 4, G) if isinstance(g, int) else g + 4)
                    pe.wait_ge(weight_t_ready, g + 1)
                    if not (isinstance(g, int) and g == 0):
                        pe.wait_ge(mixed, 2 * g)
                    nc.tensor.matmul(wsum_p, ones[:, :], weight_t[:, :], start=True, stop=True)\
                      .then_inc(wsum_mm, 1)
                else:
                    pe.wait_ge(mixed, 2 * g + 1)
                for q in range(2):
                    for odd in range(2):
                        cols = bass.ts(4 * half + 2 * q + odd, P)
                        nc.tensor.matmul(bias_p[:, odd, q, :], ebt_hi[:, cols], weight_t[:, :],
                                         start=True, stop=False)
                        ins = nc.tensor.matmul(bias_p[:, odd, q, :], ebt_lo[:, cols], weight_t[:, :],
                                               start=False, stop=True)
                ins.then_inc(bias_mm, 1)

            filters_of(0, 0, 0)
            filters_of(1, 0, 1)
            pe.wait_ge(consts_loaded, 112)
            pe.wait_ge(zeros_made, 2)
            pe.wait_ge(expert_lo_ready, 1)

            def group(g, it, k):
                if there(g):
                    convolve(g, it, k, 0, 0)
                if there(g - 2):
                    bias(g - 2, 0)
                if there(g):
                    convolve(g, it, k, 0, 1)
                if there(g - 2):
                    bias(g - 2, 1)
                if there(g - 1):
                    logits(g - 1, k - 1)
                if there(g):
                    convolve(g, it, k, 1, 0)
                if there(g + 2):
                    filters_of(g + 2, it, k + 2)
                if there(g - 1):
                    tokens(g - 1)
                if there(g):
                    convolve(g, it, k, 1, 1)
                if there(g - 1):
                    weights(g - 1)

            run(pe, group, G + 2)


def kernel(x, itok_B_78_3631, L0_cond_log_dt, L0_cond_C, L0_cond_log_A_real, L0_cond_A_imag, L0_cond_D,
           L0_ffn_router_weight, L0_ffn_router_bias, L0_ffn_expert_bias):
    import concourse.bacc as bacc
    from concourse.bass_utils import run_bass_kernel_spmd

    f32 = np.float32
    x, length = np.asarray(x), np.asarray(itok_B_78_3631)
    log_dt, c_in = np.asarray(L0_cond_log_dt), np.asarray(L0_cond_C)
    log_a, a_im, d = np.asarray(L0_cond_log_A_real), np.asarray(L0_cond_A_imag), np.asarray(L0_cond_D)
    rw, rb, eb = (np.asarray(a) for a in (L0_ffn_router_weight, L0_ffn_router_bias, L0_ffn_expert_bias))

    def twice(a):
        return np.concatenate([a.T, a.T], axis=0)

    modes = np.stack([np.broadcast_to(log_dt, (P, H)), twice(log_a), twice(a_im), twice(c_in[:, :, 0]),
                      twice(c_in[:, :, 1])], axis=1)
    steps = np.concatenate([np.arange(NI), NI * np.arange(NA), NI * np.arange(NA)])
    cosine_first = np.repeat([0.25, 0.0], N)[:, None]
    offsets = np.concatenate([np.broadcast_to(cosine_first, (P, NI + NA)),
                              np.broadcast_to(0.25 - cosine_first, (P, NA))], axis=1)
    by_group = x.reshape(B, G, 2, NC, P).transpose(1, 4, 3, 2, 0)
    sent = {
        "x": by_group.reshape(G, P, 2 * L),
        "x_rev": by_group[:, ::-1].reshape(G, P, 2 * L),
        "lens": np.broadcast_to(length, (P, B)),
        "modes": modes,
        "d_skip": d.reshape(1, H),
        "router": rw.reshape(E, NC, P).transpose(2, 1, 0),
        "router_bias": np.concatenate([rb, np.zeros(E, rb.dtype)]).reshape(P, 1),
        "expert_bias": np.concatenate([eb, eb], axis=0),
        "steps": np.broadcast_to(steps, (P, NJ)).astype(f32),
        "offsets": offsets.astype(f32),
        "l_index": (np.arange(P)[:, None] + P * np.arange(NC)[None, :]).astype(f32),
        "identity": np.eye(P, dtype=f32),
        "fold": np.concatenate([np.eye(E, dtype=f32)] * 2, axis=0),
    }
    sent = {name: np.ascontiguousarray(a) for name, a in sent.items()}

    nc = bacc.Bacc("TRN2", target_bir_lowering=False, num_devices=1)
    aps = {name: nc.dram_tensor(f"in_{name}", a.shape, mybir.dt.from_np(a.dtype), kind="ExternalInput").ap()
           for name, a in sent.items()}
    out = nc.dram_tensor("out_dram", (G, P, 2 * L), F32, kind="ExternalOutput").ap()
    build(nc, out=out, **aps)
    result = run_bass_kernel_spmd(nc, [{f"in_{name}": a for name, a in sent.items()}], core_ids=[0])
    got = result.results[0]["out_dram"]
    return got.reshape(G, P, NC, 2, B).transpose(4, 0, 3, 2, 1).reshape(B, H, L)
```

```python
from contextlib import ExitStack

import numpy as np

import concourse.bass as bass
from concourse import mybir

F32 = mybir.dt.float32
F32R = mybir.dt.float32r
I32 = mybir.dt.int32
ALU = mybir.AluOpType
ACT = mybir.ActivationFunctionType

P = 128
B, H, L = 128, 64, 1024
N, E, TOP = 64, 64, 8
NC = L // P
HALF = NC // 2
G = H // 2
UNROLL = 4
HB = 2 * UNROLL
NI, NA = 64, L // 64
NJ = NI + 2 * NA
ROW = P + L

ROUND = 1.5 * 2.0 ** 23
ROUND18 = 1.5 * 2.0 ** 5
TWO_PI = 6.283184
LOWEST = -3.4028235e38
LN2_HI, LN2_LO = 0.693359375, -2.12194440e-4
LOG2_E = 1.4426950408889634
EXP_SERIES = (1.0 / 5040, 1.0 / 720, 1.0 / 120, 1.0 / 24, 1.0 / 6, 0.5, 1.0)


def inverse_two_pi_parts():
    x = 1.0 / (2.0 * np.pi)
    c1 = np.round(x * 2 ** 14) / 2 ** 14
    c2 = np.round((x - c1) * 2 ** 26) / 2 ** 26
    return float(c1), float(c2), float(x - c1 - c2)


def build(nc, x, x_rev, lens, modes, d_skip, router, router_bias, expert_bias, steps, offsets, l_index,
          identity, fold, out):
    ctx = ExitStack()
    with ctx:
        def sb(name, shape, dt=F32):
            return ctx.enter_context(nc.sbuf_tensor(name, shape, dt))

        def ps(name, shape):
            return ctx.enter_context(nc.psum_tensor(name, shape, F32))

        def sem(name):
            return ctx.enter_context(nc.semaphore(name))

        filters = nc.dram_tensor("filters", [H, ROW], F32, kind="Internal").ap()
        toeplitz = bass.AP(filters.tensor, filters.offset + 1, [[ROW, H], [1, P], [1, L]])

        xs = [sb(f"xs{i}", [P, NC, 2, B]) for i in range(2)]
        us = [sb(f"us{i}", [P, NC, 2, B]) for i in range(2)]
        u_hi = [sb(f"u_hi{i}", [P, NC, 2, B], F32R) for i in range(2)]
        u_lo = [sb(f"u_lo{i}", [P, NC, 2, B], F32R) for i in range(2)]
        toe = [sb(f"toe{i}", [P, L]) for i in range(4)]
        toe_hi = [sb(f"toe_hi{i}", [P, L], F32R) for i in range(2)]
        toe_lo = [sb(f"toe_lo{i}", [P, L], F32R) for i in range(2)]
        zs = [sb(f"zs{i}", [P, NC, 2, B]) for i in range(4)]
        mask = sb("mask", [P, NC, B])
        len_i = sb("len_i", [P, B], I32)
        len_f = sb("len_f", [P, B])
        l_idx = sb("l_idx", [P, NC])
        rwt = sb("rwt", [P, NC, E])
        rbias = sb("rbias", [P, 1])
        ebt = sb("ebt", [P, L])
        ebt_hi = sb("ebt_hi", [P, L], F32R)
        ebt_lo = sb("ebt_lo", [P, L], F32R)
        ident = sb("ident", [P, P])
        fold_sb = sb("fold_sb", [P, E])
        ones = sb("ones", [P, P], F32R)
        logit_t = sb("logit_t", [P, 2 * B])
        token = sb("token", [P, 2, E])
        top8 = sb("top8", [P, 2, TOP])
        neg_max = sb("neg_max", [P, 2])
        escore = sb("escore", [P, 2, E])
        esum = sb("esum", [P, 2])
        rsum = sb("rsum", [P, 2])
        dropped = sb("dropped", [P, 2, E])
        kept = sb("kept", [P, 2, E])
        weight2 = sb("weight2", [P, 2, 2, E])
        weight_t = sb("weight_t", [P, 2 * B], F32R)
        md = sb("md", [P, 5, H])
        dsk = sb("dsk", [1, H])
        st = sb("st", [P, NJ])
        off = sb("off", [P, NJ])
        cx = sb("cx", [P, 26, H])
        qx = sb("qx", [P, 6, H])
        cb_hi = sb("cb_hi", [P, H], F32R)
        ci = sb("ci", [P, 2, H], I32)
        turn_hi = sb("turn_hi", [P, H])
        turn_lo = sb("turn_lo", [P, H])
        decay = sb("decay", [P, H])
        coef_own = sb("coef_own", [P, H])
        coef_oth = sb("coef_oth", [P, H])
        ph = sb("ph", [P, HB, NJ])
        ph_int = sb("ph_int", [P, HB, NJ])
        ph_lo = sb("ph_lo", [P, HB, NJ])
        dec = sb("dec", [P, HB, NI + NA])
        sn = sb("sn", [P, HB, NJ])
        ex = sb("ex", [P, HB, NI + NA])
        w_own = sb("w_own", [P, HB, NA])
        w_oth = sb("w_oth", [P, HB, NA])
        tab_v = sb("tab_v", [P, HB, NI])
        tab_w = sb("tab_w", [P, HB, NA])
        k_sb = sb("k_sb", [NA, 2, NI])
        zeros = sb("zeros", [H, P])

        y = [ps(f"y{i}", [P, NC, B]) for i in range(2)]
        bank_t = ps("bank_t", [P, 512])
        bank_s = ps("bank_s", [P, 512])
        bias_p = ps("bias_p", [P, 2, 2, 2 * B])
        logit_p = bank_t[:, 0:256]
        weight_p = bank_t[:, 256:512]
        token_p = bank_s[:, 0:128]
        wsum_p = bank_s[:, 128:384]
        filter_p = bank_s[0:NA, 384:512]

        x_loaded = [sem(f"x_loaded{i}") for i in range(2)]
        u_loaded = [sem(f"u_loaded{i}") for i in range(2)]
        toe_loaded = [sem(f"toe_loaded{i}") for i in range(4)]
        out_stored = [sem(f"out_stored{i}") for i in range(4)]
        modes_loaded = sem("modes_loaded")
        steps_loaded = sem("steps_loaded")
        consts_loaded = sem("consts_loaded")
        zeros_made = sem("zeros_made")
        pad_written = sem("pad_written")
        filter_written = sem("filter_written")
        const_step = sem("const_step")
        const_hi = sem("const_hi")
        mask_ready = sem("mask_ready")
        quotient_step = sem("quotient_step")
        exps_ready = sem("exps_ready")
        turns_ready = sem("turns_ready")
        head_pool = sem("head_pool")
        head_dve = sem("head_dve")
        head_act = sem("head_act")
        tab_pool = sem("tab_pool")
        tab_dve = sem("tab_dve")
        tab_act = sem("tab_act")
        filter_mm = sem("filter_mm")
        k_copied = sem("k_copied")
        k_full = sem("k_full")
        toe_hi_ready = sem("toe_hi_ready")
        toe_lo_ready = sem("toe_lo_ready")
        u_hi_ready = sem("u_hi_ready")
        u_lo_ready = sem("u_lo_ready")
        conv_half = sem("conv_half")
        z_half = sem("z_half")
        logits_mm = sem("logits_mm")
        logit_t_ready = sem("logit_t_ready")
        token_mm = sem("token_mm")
        token_ready = sem("token_ready")
        max_step = sem("max_step")
        exp_done = sem("exp_done")
        drop_done = sem("drop_done")
        kept_step = sem("kept_step")
        weights_ready = sem("weights_ready")
        weight_mm = sem("weight_mm")
        weight_hi_ready = sem("weight_hi_ready")
        weight_t_ready = sem("weight_t_ready")
        expert_hi_ready = sem("expert_hi_ready")
        expert_lo_ready = sem("expert_lo_ready")
        wsum_mm = sem("wsum_mm")
        bias_mm = sem("bias_mm")
        scaled = sem("scaled")
        mixed = sem("mixed")
        final = sem("final")

        block = ctx.enter_context(nc.Block())

        def run(eng, group, last):
            for g in range(UNROLL):
                group(g, 0, g)
            with eng.Fori(1, G // UNROLL - 1, 1) as it:
                for k in range(UNROLL):
                    group(it * UNROLL + k, it, k)
            for g in range(G - UNROLL, last):
                group(g, g // UNROLL, g % UNROLL)

        def there(g):
            return 0 <= g < G if isinstance(g, int) else True

        @block.sync
        def _(sp):
            sp.dma_start(md[:, :, :], modes).then_inc(modes_loaded, 16)
            sp.dma_start(us[0][:, :, :, :], x_rev[0]).then_inc(u_loaded[0], 16)
            sp.dma_start(st[:, :], steps).then_inc(steps_loaded, 16)
            sp.dma_start(off[:, :], offsets).then_inc(steps_loaded, 16)
            sp.dma_start(dsk[:, :], d_skip).then_inc(steps_loaded, 16)
            sp.dma_start(len_i[:, :], lens).then_inc(consts_loaded, 16)
            sp.dma_start(l_idx[:, :], l_index).then_inc(consts_loaded, 16)
            sp.dma_start(rwt[:, :, :], router).then_inc(consts_loaded, 16)
            sp.dma_start(rbias[:, :], router_bias).then_inc(consts_loaded, 16)
            sp.dma_start(ebt[:, :], expert_bias).then_inc(consts_loaded, 16)
            sp.dma_start(ident[:, :], identity).then_inc(consts_loaded, 16)
            sp.dma_start(fold_sb[:, :], fold).then_inc(consts_loaded, 16)
            sp.dma_start(us[1][:, :, :, :], x_rev[1]).then_inc(u_loaded[1], 16)
            sp.wait_ge(zeros_made, 1)
            sp.dma_start(filters[:, 0:P], zeros[:, :]).then_inc(pad_written, 16)

            def write_filter(g):
                sp.wait_ge(k_full, g + 1)
                sp.dma_start(filters[bass.ts(g, 2), P:ROW].rearrange("s (a i) -> a s i", a=NA), k_sb[:, :, :])\
                  .then_inc(filter_written, 16)

            def load_toeplitz(g, k):
                for j in range(2):
                    slot = (2 * k + j) % 4
                    if not (isinstance(g, int) and g < 2):
                        sp.wait_ge(toe_lo_ready, 2 * g + j - 3)
                    if j == 0:
                        sp.wait_ge(filter_written, 16 * g + 16)
                    sp.dma_start(toe[slot][:, :], toeplitz[2 * g + j]).then_inc(toe_loaded[slot], 16)

            sp.wait_ge(pad_written, 16)
            write_filter(0)
            load_toeplitz(0, 0)
            write_filter(1)

            def group(g, it, k):
                if there(g + 2):
                    sp.wait_ge(u_lo_ready, g + 1)
                    sp.dma_start(us[k % 2][:, :, :, :], x_rev[g + 2]).then_inc(u_loaded[k % 2], 16)
                if there(g + 1):
                    load_toeplitz(g + 1, k + 1)
                if there(g - 2):
                    for half in range(2):
                        sp.wait_ge(final, 2 * g - 3 + half)
                        cs = slice(half * HALF, (half + 1) * HALF)
                        sp.dma_start(out[g - 2].rearrange("p (c n) -> p c n", c=NC)[:, cs, :],
                                     zs[(k - 2) % 4][:, cs, :, :].rearrange("p c j b -> p c (j b)"))\
                          .then_inc(out_stored[(k - 2) % 4], 16)
                if there(g):
                    sp.dma_start(xs[k % 2][:, :, :, :], x[g]).then_inc(x_loaded[k % 2], 16)
                if there(g + 2):
                    write_filter(g + 2)

            run(sp, group, G + 2)
            for i in range(4):
                sp.wait_ge(out_stored[i], 32 * (G // 4))

        @block.gpsimd
        def _(pool):
            nc.gpsimd.memset(zeros[:, :], 0.0).then_inc(zeros_made, 1)
            nc.gpsimd.memset(ones[:, :].bitcast(F32), 1.0).then_inc(zeros_made, 1)

            def tables(nb, c0=0, c1=HB, done=tab_pool):
                n = c1 - c0
                hs = slice(c0, c1) if isinstance(nb, int) and nb == 0 else bass.ts(nb, HB)
                if not (isinstance(nb, int) and nb == 0):
                    pool.wait_ge(tab_dve, 10 * nb)

                def along_steps(a, width=NJ):
                    return a[:, hs].unsqueeze(2).broadcast_to([P, n, width])

                def for_channels(a, width=NJ):
                    return a[:, 0:width].unsqueeze(1).broadcast_to([P, n, width])

                nc.gpsimd.tensor_tensor(ph[:, c0:c1, :], along_steps(turn_hi), for_channels(st), ALU.mult)\
                  .then_inc(done, 1)
                nc.gpsimd.tensor_tensor(ph_lo[:, c0:c1, :], along_steps(turn_lo), for_channels(st), ALU.mult)\
                  .then_inc(done, 1)
                pool.wait_ge(done, 4 * nb + 1)
                nc.gpsimd.tensor_tensor(ph[:, c0:c1, :], ph[:, c0:c1, :], for_channels(off), ALU.add)\
                  .then_inc(done, 1)
                nc.gpsimd.tensor_tensor(dec[:, c0:c1, :], along_steps(decay, NI + NA), for_channels(st, NI + NA),
                                        ALU.mult).then_inc(done, 1)

            def residual(g, it, k, half):
                cs = slice(half * HALF, (half + 1) * HALF)
                pool.wait_ge(x_loaded[k % 2], 32 * it + 16 * (k // 2) + 16)
                pool.wait_ge(mixed, 2 * g + half + 1)
                nc.gpsimd.tensor_tensor(zs[k % 4][:, cs, :, :], zs[k % 4][:, cs, :, :], xs[k % 2][:, cs, :, :],
                                        ALU.add).then_inc(final, 1)

            def split_toeplitz(g, k, j):
                pool.wait_ge(toe_hi_ready, 2 * g + j + 1)
                nc.gpsimd.tensor_tensor(toe_lo[j][:, :], toe[(2 * k + j) % 4][:, :], toe_hi[j][:, :].bitcast(F32),
                                        ALU.subtract).then_inc(toe_lo_ready, 1)

            def step(n, o, a, b, op):
                if n:
                    pool.wait_ge(quotient_step, n)
                nc.gpsimd.tensor_tensor(o, a, b, op).then_inc(quotient_step, 1)

            pool.wait_ge(modes_loaded, 16)
            pool.wait_ge(exps_ready, 1)
            are, aim, c_re, c_im = cx[:, 13, :], md[:, 2, :], md[:, 3, :], md[:, 4, :]
            q = [qx[:, i, :] for i in range(6)]
            step(0, q[0], are, are, ALU.mult)
            step(1, q[1], aim, aim, ALU.mult)
            step(2, q[0], q[0], q[1], ALU.add)
            step(3, q[2], c_im, aim, ALU.mult)
            step(4, q[3], c_re, are, ALU.mult)
            step(5, q[2], q[2], q[3], ALU.subtract)
            step(6, q[4], c_im, are, ALU.mult)
            step(7, q[5], c_re, aim, ALU.mult)
            step(8, q[4], q[4], q[5], ALU.add)
            pool.wait_ge(turns_ready, 1)
            pool.wait_ge(steps_loaded, 48)
            tables(0, 0, 2, head_pool)
            tables(0, 2, HB)
            pool.wait_ge(u_hi_ready, 1)
            nc.gpsimd.tensor_tensor(u_lo[0][:, :, :, :], us[0][:, :, :, :], u_hi[0][:, :, :, :].bitcast(F32),
                                    ALU.subtract).then_inc(u_lo_ready, 1)
            pool.wait_ge(toe_lo_ready, 1)

            def group(g, it, k):
                if there(g):
                    split_toeplitz(g, k, 1)
                if there(g - 2):
                    residual(g - 2, it, k - 2, 0)
                if there(g + 1):
                    split_toeplitz(g + 1, k + 1, 0)
                if there(g - 2):
                    residual(g - 2, it, k - 2, 1)
                if k == 0 and there(g + UNROLL):
                    tables(it + 1)

            run(pool, group, G + 2)

        @block.scalar
        def _(act):
            def split(g, it, k):
                act.wait_ge(u_loaded[k % 2], 32 * it + 16 * (k // 2) + 16)
                if not (isinstance(g, int) and g < 2):
                    act.wait_ge(conv_half, 4 * g - 4)
                nc.scalar.activation(u_hi[k % 2][:, :, :, :], us[k % 2][:, :, :, :], ACT.Copy)\
                  .then_inc(u_hi_ready, 1)

            def tables(nb, c0=0, c1=HB, from_pool=tab_pool, from_dve=tab_dve, done=tab_act):
                act.wait_ge(from_dve, 10 * nb + 5)
                nc.scalar.activation(sn[:, c0:c1, :], ph[:, c0:c1, :], ACT.Sin, scale=TWO_PI).then_inc(done, 1)
                act.wait_ge(from_pool, 4 * nb + 4)
                nc.scalar.activation(ex[:, c0:c1, :], dec[:, c0:c1, :], ACT.Exp).then_inc(done, 1)

            def take_filter(g):
                if not (isinstance(g, int) and g == 0):
                    act.wait_ge(filter_written, 16 * g)
                act.wait_ge(filter_mm, g + 1)
                nc.scalar.activation(k_sb[:, :, :].rearrange("a j i -> a (j i)"), filter_p, ACT.Copy)\
                  .then_inc(k_copied, 1)

            def split_toeplitz(g, it, k, j):
                slot = (2 * k + j) % 4
                act.wait_ge(toe_loaded[slot], 32 * it + 16 * ((2 * k + j) // 4) + 16)
                if not (isinstance(g, int) and g == 0):
                    act.wait_ge(conv_half, 4 * g + 2 * j - 2)
                nc.scalar.activation(toe_hi[j][:, :], toe[slot][:, :], ACT.Copy).then_inc(toe_hi_ready, 1)

            act.wait_ge(const_hi, 1)
            nc.scalar.activation(cb_hi[:, :], cx[:, 0, :], ACT.Copy).then_inc(const_hi, 1)
            split(0, 0, 0)
            act.wait_ge(const_hi, 3)
            nc.scalar.activation(cx[:, 10, :], cx[:, 9, :], ACT.Sin, scale=TWO_PI).then_inc(const_hi, 1)
            nc.scalar.activation(cx[:, 11, :], cx[:, 9, :], ACT.Sin, scale=TWO_PI / 2).then_inc(const_hi, 1)
            tables(0, 0, 2, head_pool, head_dve, head_act)
            take_filter(0)
            tables(0, 2)
            act.wait_ge(consts_loaded, 112)
            nc.scalar.activation(ebt_hi[:, :], ebt[:, :], ACT.Copy).then_inc(expert_hi_ready, 1)
            take_filter(1)
            split_toeplitz(0, 0, 0, 0)

            def group(g, it, k):
                if there(g - 2):
                    act.wait_ge(weight_mm, g - 1)
                    if not (isinstance(g, int) and g == 2):
                        act.wait_ge(bias_mm, 2 * (g - 2))
                    nc.scalar.activation(weight_t[:, :], weight_p, ACT.Copy).then_inc(weight_hi_ready, 1)
                if there(g):
                    split_toeplitz(g, it, k, 1)
                if there(g - 1):
                    act.wait_ge(logits_mm, g)
                    nc.scalar.activation(logit_t[:, :], logit_p, ACT.Identity, bias=rbias[:, 0:1])\
                      .then_inc(logit_t_ready, 1)
                if there(g + 1):
                    split(g + 1, it, k + 1)
                if k == 2 and there(g + UNROLL - k):
                    tables(it + 1)
                if there(g - 1):
                    act.wait_ge(token_mm, g)
                    if not (isinstance(g, int) and g == 1):
                        act.wait_ge(weights_ready, g - 1)
                    nc.scalar.activation(token[:, :, :].rearrange("p j e -> p (j e)"), token_p, ACT.Copy)\
                      .then_inc(token_ready, 1)
                if there(g + 1):
                    split_toeplitz(g + 1, it, k + 1, 0)
                if there(g - 1):
                    act.wait_ge(max_step, 3 * g)
                    for j in range(2):
                        ins = nc.scalar.activation(escore[:, j, :], token[:, j, :], ACT.Exp,
                                                   bias=neg_max[:, j:j + 1], accum_out=esum[:, j:j + 1])
                    ins.then_inc(exp_done, 1)
                if there(g + 2):
                    take_filter(g + 2)

            run(act, group, G + 2)

        @block.vector
        def _(dve):
            steps_done = [0]

            def link(ins, behind=0):
                steps_done[0] += 1
                ins.then_inc(const_step, 1)
                dve.wait_ge(const_step, steps_done[0] - behind)

            def tt(o, a, b, op, behind=0):
                link(nc.vector.tensor_tensor(o, a, b, op), behind)

            def ts(o, a, s1, s2, op0, op1, behind=0):
                link(nc.vector.tensor_scalar(o, a, s1, s2, op0, op1), behind)

            def stt(o, a, s, b, op0, op1, behind=0):
                link(nc.vector.scalar_tensor_tensor(o, a, s, b, op0, op1), behind)

            steady = (tab_pool, tab_dve, tab_act)
            head = (head_pool, head_dve, head_act)

            def reduce_phases(nb, c0, c1, from_pool, done, from_act, steps):
                t, whole, low = (a[:, c0:c1, :] for a in (ph, ph_int, ph_lo))
                for n in steps:
                    if n == 0:
                        dve.wait_ge(from_pool, 4 * nb + 3)
                    else:
                        dve.wait_ge(done, 10 * nb + n)
                    if n in (0, 3):
                        ins = nc.vector.tensor_scalar(whole, t, ROUND, ROUND, ALU.add, ALU.subtract)
                    elif n in (1, 4):
                        ins = nc.vector.tensor_tensor(t, t, whole, ALU.subtract)
                    else:
                        ins = nc.vector.tensor_tensor(t, t, low, ALU.add)
                    ins.then_inc(done, 1)

            def make_tables(nb, c0, c1, from_pool, done, from_act):
                n = c1 - c0
                hs = slice(c0, c1) if isinstance(nb, int) and nb == 0 else bass.ts(nb, HB)
                dve.wait_ge(from_act, 2 * nb + 2)
                if not (isinstance(nb, int) and nb == 0):
                    dve.wait_ge(filter_mm, UNROLL * nb)
                nc.vector.tensor_tensor(tab_v[:, c0:c1, :], sn[:, c0:c1, 0:NI], ex[:, c0:c1, 0:NI], ALU.mult)\
                  .then_inc(done, 1)
                nc.vector.tensor_tensor(w_own[:, c0:c1, :], sn[:, c0:c1, NI:NI + NA],
                                        coef_own[:, hs].unsqueeze(2).broadcast_to([P, n, NA]), ALU.mult)\
                  .then_inc(done, 1)
                nc.vector.tensor_tensor(w_oth[:, c0:c1, :], sn[:, c0:c1, NI + NA:NJ],
                                        coef_oth[:, hs].unsqueeze(2).broadcast_to([P, n, NA]), ALU.mult)\
                  .then_inc(done, 1)
                dve.wait_ge(done, 10 * nb + 8)
                nc.vector.tensor_tensor(w_own[:, c0:c1, :], w_own[:, c0:c1, :], w_oth[:, c0:c1, :], ALU.add)\
                  .then_inc(done, 1)
                dve.wait_ge(done, 10 * nb + 9)
                nc.vector.tensor_tensor(tab_w[:, c0:c1, :], w_own[:, c0:c1, :], ex[:, c0:c1, NI:NI + NA], ALU.mult)\
                  .then_inc(done, 1)

            c = [cx[:, i, :] for i in range(26)]
            dve.wait_ge(modes_loaded, 16)
            pair_x, pair_k, pair_r, pair_q = md[:, 0:2, :], cx[:, 14:16, :], cx[:, 16:18, :], cx[:, 18:20, :]
            ts(pair_k, pair_x, LOG2_E, ROUND, ALU.mult, ALU.add)
            ts(pair_k, pair_k, ROUND, None, ALU.subtract, ALU.bypass)
            ts(pair_k, pair_k, -126.0, 127.0, ALU.max, ALU.min)
            stt(pair_r, pair_k, -LN2_HI, pair_x, ALU.mult, ALU.add)
            stt(pair_r, pair_k, -LN2_LO, pair_r, ALU.mult, ALU.add)
            ts(pair_q, pair_r, EXP_SERIES[0], None, ALU.mult, ALU.bypass)
            for term in EXP_SERIES[1:-1]:
                stt(pair_q, pair_q, term, pair_r, ALU.add, ALU.mult)
            ts(ci[:, :, :], pair_k, 127.0, 2.0 ** 23, ALU.add, ALU.mult, behind=1)
            stt(pair_q, pair_q, EXP_SERIES[-1], pair_r, ALU.add, ALU.mult)
            stt(cx[:, 12:14, :], pair_q, 1.0, ci[:, :, :].bitcast(F32), ALU.add, ALU.mult)
            dt, are, aim = cx[:, 12, :], cx[:, 13, :], md[:, 2, :]
            dve.sem_inc(exps_ready, 1)
            tt(c[0], aim, dt, ALU.mult)
            dve.sem_inc(const_hi, 1)
            stt(decay[:, :], are, -1.0, dt, ALU.mult, ALU.mult)
            c1, c2, c3 = inverse_two_pi_parts()
            bh = cb_hi[:, :].bitcast(F32)
            k, rest, q, two_k = c[14], c[15], c[16], ci[:, 0, :].bitcast(F32)
            ts(k, decay[:, :], LOG2_E, ROUND, ALU.mult, ALU.add)
            ts(k, k, ROUND, None, ALU.subtract, ALU.bypass)
            dve.wait_ge(const_hi, 2)
            tt(c[1], c[0], bh, ALU.subtract, behind=1)
            ts(k, k, -126.0, 127.0, ALU.max, ALU.min, behind=1)
            ts(c[2], bh, c1, None, ALU.mult, ALU.bypass, behind=1)
            stt(rest, k, -LN2_HI, decay[:, :], ALU.mult, ALU.add, behind=1)
            ts(c[3], c[2], ROUND, ROUND, ALU.add, ALU.subtract, behind=1)
            stt(rest, k, -LN2_LO, rest, ALU.mult, ALU.add, behind=1)
            tt(c[2], c[2], c[3], ALU.subtract, behind=1)
            ts(ci[:, 0, :], k, 127.0, 2.0 ** 23, ALU.add, ALU.mult, behind=1)
            ts(c[4], c[1], c1, None, ALU.mult, ALU.bypass, behind=1)
            ts(q, rest, EXP_SERIES[0], None, ALU.mult, ALU.bypass, behind=1)
            tt(c[3], c[2], c[4], ALU.add, behind=1)
            stt(q, q, EXP_SERIES[1], rest, ALU.add, ALU.mult, behind=1)
            ts(c[5], bh, c2, None, ALU.mult, ALU.bypass)
            tt(c[3], c[3], c[5], ALU.add, behind=1)
            stt(q, q, EXP_SERIES[2], rest, ALU.add, ALU.mult, behind=1)
            ts(turn_hi[:, :], c[3], ROUND18, ROUND18, ALU.add, ALU.subtract, behind=1)
            stt(q, q, EXP_SERIES[3], rest, ALU.add, ALU.mult, behind=1)
            tt(c[2], c[2], turn_hi[:, :], ALU.subtract, behind=1)
            stt(q, q, EXP_SERIES[4], rest, ALU.add, ALU.mult, behind=1)
            tt(c[2], c[2], c[4], ALU.add, behind=1)
            stt(q, q, EXP_SERIES[5], rest, ALU.add, ALU.mult, behind=1)
            tt(c[2], c[2], c[5], ALU.add, behind=1)
            stt(q, q, EXP_SERIES[6], rest, ALU.add, ALU.mult, behind=1)
            stt(c[2], bh, c3, c[2], ALU.mult, ALU.add, behind=1)
            tt(c[18], q, two_k, ALU.mult, behind=1)
            stt(turn_lo[:, :], c[1], c2, c[2], ALU.mult, ALU.add, behind=1)
            stt(c[17], q, 1.0, two_k, ALU.add, ALU.mult)
            dve.sem_inc(turns_ready, 1)
            tt(c[8], turn_hi[:, :], turn_lo[:, :], ALU.add, behind=1)
            stt(c[18], two_k, -1.0, c[18], ALU.add, ALU.add, behind=1)
            ts(c[7], c[8], ROUND, ROUND, ALU.add, ALU.subtract)
            tt(c[9], c[8], c[7], ALU.subtract)
            dve.sem_inc(const_hi, 1)
            dve.wait_ge(quotient_step, 9)
            link(nc.vector.reciprocal(c[24], qx[:, 0, :]))
            tt(c[25], qx[:, 2, :], c[24], ALU.mult, behind=1)
            tt(c[6], qx[:, 4, :], c[24], ALU.mult, behind=1)
            dve.wait_ge(const_hi, 5)
            stt(c[19], c[11], -2.0, c[11], ALU.mult, ALU.mult, behind=1)
            tt(c[21], c[17], c[10], ALU.mult, behind=1)
            tt(c[20], c[19], c[17], ALU.mult)
            tt(c[5], c[6], c[21], ALU.mult, behind=1)
            tt(c[20], c[20], c[18], ALU.add, behind=1)
            reduce_phases(0, 0, 2, *head, steps=(0,))
            tt(c[7], c[25], c[21], ALU.mult, behind=1)
            tt(c[3], c[25], c[20], ALU.mult, behind=1)
            reduce_phases(0, 0, 2, *head, steps=(1,))
            tt(c[8], c[6], c[20], ALU.mult, behind=1)
            reduce_phases(0, 0, 2, *head, steps=(2,))
            tt(c[22], c[3], c[5], ALU.add, behind=1)
            reduce_phases(0, 0, 2, *head, steps=(3,))
            tt(c[23], c[8], c[7], ALU.subtract, behind=1)
            reduce_phases(0, 0, 2, *head, steps=(4,))
            ts(coef_own[0:N, :], cx[0:N, 22, :], 2.0, None, ALU.mult, ALU.bypass, behind=1)
            ts(coef_own[N:P, :], cx[N:P, 22, :], -2.0, None, ALU.mult, ALU.bypass, behind=1)
            ts(coef_oth[:, :], c[23], 2.0, None, ALU.mult, ALU.bypass)

            def add_skip(g):
                dve.wait_ge(k_copied, g + 1)
                nc.vector.tensor_tensor(k_sb[0:1, :, 0], k_sb[0:1, :, 0], dsk[0:1, bass.ts(g, 2)], ALU.add)\
                  .then_inc(k_full, 1)

            def split(g, k):
                dve.wait_ge(u_hi_ready, g + 1)
                nc.vector.tensor_tensor(u_lo[k % 2][:, :, :, :], us[k % 2][:, :, :, :],
                                        u_hi[k % 2][:, :, :, :].bitcast(F32), ALU.subtract)\
                  .then_inc(u_lo_ready, 1)

            def masked(g, it, k, j, half):
                cs = slice(half * HALF, (half + 1) * HALF)
                if j == 0 and half == 0 and not (isinstance(g, int) and g < 4):
                    dve.wait_ge(out_stored[k], 32 * it)
                dve.wait_ge(conv_half, 4 * g + 2 * j + half + 1)
                nc.vector.tensor_tensor(zs[k][:, cs, j, :], y[j][:, cs, :], mask[:, cs, :], ALU.mult)\
                  .then_inc(z_half, 1)

            def softmax(g):
                for j in range(2):
                    nc.vector.max(top8[:, j, :], token[:, j, :]).then_inc(max_step, 1)
                dve.wait_ge(max_step, 3 * g + 2)
                nc.vector.tensor_scalar(neg_max[:, :], top8[:, :, 0], -1.0, None, ALU.mult, ALU.bypass)\
                  .then_inc(max_step, 1)
                for j in range(2):
                    ins = nc.vector.match_replace(out=dropped[:, j, :], in_to_replace=top8[:, j, :],
                                                  in_values=token[:, j, :], imm_value=LOWEST)
                ins.then_inc(drop_done, 1)
                dve.wait_ge(exp_done, g + 1)
                nc.vector.reciprocal(rsum[:, :], esum[:, :]).then_inc(kept_step, 1)
                dve.wait_ge(drop_done, g + 1)
                nc.vector.scalar_tensor_tensor(kept[:, :, :], dropped[:, :, :], LOWEST, escore[:, :, :],
                                               ALU.is_equal, ALU.mult).then_inc(kept_step, 1)
                dve.wait_ge(kept_step, 2 * g + 2)
                if not (isinstance(g, int) and g == 0):
                    dve.wait_ge(weight_mm, g)
                nc.vector.tensor_tensor(weight2[:, :, :, :], kept[:, :, :].unsqueeze(2).broadcast_to([P, 2, 2, E]),
                                        rsum[:, :].unsqueeze(2).unsqueeze(3).broadcast_to([P, 2, 2, E]), ALU.mult)\
                  .then_inc(weights_ready, 1)

            def low_weights(g):
                dve.wait_ge(weight_hi_ready, g + 1)
                nc.vector.tensor_tensor(weight_t[E:P, :], weight_p[E:P, :], weight_t[E:P, :].bitcast(F32),
                                        ALU.subtract).then_inc(weight_t_ready, 1)

            def scale(g, k, half):
                dve.wait_ge(wsum_mm, g + 1)
                zv = zs[k % 4][:, half * HALF:(half + 1) * HALF, :, :].rearrange("p c j b -> p c (j b)")
                nc.vector.tensor_tensor(zv, zv, wsum_p.unsqueeze(1).broadcast_to([P, HALF, 2 * B]), ALU.mult)\
                  .then_inc(scaled, 1)

            def mix(g, k, half):
                cs = slice(half * HALF, (half + 1) * HALF)
                dve.wait_ge(scaled, 2 * g + half + 1)
                dve.wait_ge(bias_mm, 2 * g + half + 1)
                zv = zs[k % 4][:, cs, :, :].rearrange("p (q t) j b -> p q t (j b)", t=2)
                nc.vector.tensor_tensor(zv, zv, bias_p[:, :, :, :].rearrange("p t q n -> p q t n"), ALU.add)\
                  .then_inc(mixed, 1)

            make_tables(0, 0, 2, *head)
            reduce_phases(0, 2, HB, *steady, steps=(0, 1, 2))
            add_skip(0)
            reduce_phases(0, 2, HB, *steady, steps=(3, 4))
            dve.wait_ge(consts_loaded, 112)
            nc.vector.tensor_copy(len_f[:, :], len_i[:, :]).then_inc(mask_ready, 1)
            dve.wait_ge(mask_ready, 1)
            for cc in range(NC):
                nc.vector.tensor_scalar(mask[:, cc, :], len_f[:, :], l_idx[:, cc:cc + 1], None, ALU.is_gt,
                                        ALU.bypass).then_inc(mask_ready, 1)
            dve.wait_ge(mask_ready, 1 + NC)
            dve.wait_ge(expert_hi_ready, 1)
            nc.vector.tensor_tensor(ebt_lo[:, :], ebt[:, :], ebt_hi[:, :].bitcast(F32), ALU.subtract)\
              .then_inc(expert_lo_ready, 1)
            make_tables(0, 2, HB, *steady)
            add_skip(1)
            dve.wait_ge(toe_hi_ready, 1)
            nc.vector.tensor_tensor(toe_lo[0][:, :], toe[0][:, :], toe_hi[0][:, :].bitcast(F32), ALU.subtract)\
              .then_inc(toe_lo_ready, 1)

            def group(g, it, k):
                tables_next = there(g + UNROLL - k)
                if there(g - 2):
                    low_weights(g - 2)
                if there(g):
                    masked(g, it, k, 0, 0)
                if there(g - 2):
                    scale(g - 2, k - 2, 0)
                    mix(g - 2, k - 2, 0)
                    scale(g - 2, k - 2, 1)
                if tables_next and k == 1:
                    reduce_phases(it + 1, 0, HB, *steady, steps=(0, 1))
                if there(g + 1):
                    split(g + 1, k + 1)
                if there(g):
                    masked(g, it, k, 0, 1)
                if tables_next and k == 2:
                    make_tables(it + 1, 0, HB, *steady)
                if there(g - 1):
                    dve.wait_ge(token_ready, g)
                if there(g - 2):
                    mix(g - 2, k - 2, 1)
                if there(g - 1):
                    softmax(g - 1)
                if tables_next and k == 1:
                    reduce_phases(it + 1, 0, HB, *steady, steps=(2, 3, 4))
                if there(g):
                    masked(g, it, k, 1, 0)
                if there(g + 2):
                    add_skip(g + 2)
                if there(g):
                    masked(g, it, k, 1, 1)

            run(dve, group, G + 2)

        @block.tensor
        def _(pe):
            def filters_of(g, it, k):
                if isinstance(g, int) and g == 0:
                    pe.wait_ge(head_dve, 10)
                else:
                    pe.wait_ge(tab_dve, 10 * (it + k // UNROLL) + 10)
                    pe.wait_ge(k_copied, g)
                if not (isinstance(g, int) and g < 4):
                    pe.wait_ge(scaled, 2 * g - 6)
                if not (isinstance(g, int) and g < 3):
                    pe.wait_ge(token_ready, g - 2)
                for j in range(2):
                    hb = 2 * (k % UNROLL) + j
                    ins = nc.tensor.matmul(filter_p[:, j * NI:(j + 1) * NI], tab_w[:, hb, :], tab_v[:, hb, :],
                                           start=True, stop=True)
                ins.then_inc(filter_mm, 1)

            def convolve(g, it, k, j, half):
                first = HALF * half
                if half == 0:
                    pe.wait_ge(toe_lo_ready, 2 * g + j + 1)
                    if j == 0:
                        pe.wait_ge(u_lo_ready, g + 1)
                if not (isinstance(g, int) and g == 0):
                    pe.wait_ge(z_half, 4 * g + 2 * j + half - 3)
                parts = ((toe_hi[j], u_hi[k % 2]), (toe_hi[j], u_lo[k % 2]), (toe_lo[j], u_hi[k % 2]))
                work = [(0, 0)] + [(d, p) for d in range(1, first + HALF) for p in range(3)] + [(0, 1), (0, 2)]
                for n, (d, p) in enumerate(work):
                    tile, u = parts[p]
                    lo, hi = max(first, d), first + HALF
                    ins = nc.tensor.matmul(y[j][:, lo:hi, :], tile[:, d * P:(d + 1) * P],
                                           u[:, lo - d:hi - d, j, :], start=(n == 0), stop=(n == len(work) - 1))
                ins.then_inc(conv_half, 1)

            def logits(g, k):
                pe.wait_ge(z_half, 4 * g + 4)
                if not (isinstance(g, int) and g == 0):
                    pe.wait_ge(logit_t_ready, g)
                    pe.wait_ge(weight_t_ready, g)
                for q in range(NC // 2):
                    for odd in range(2):
                        ins = nc.tensor.matmul(logit_p[odd * E:(odd + 1) * E, :], rwt[:, 2 * q + odd, :],
                                               zs[k % 4][:, 2 * q + odd, :, :], start=(q == 0),
                                               stop=(q == NC // 2 - 1))
                ins.then_inc(logits_mm, 1)

            def tokens(g):
                pe.wait_ge(logit_t_ready, g + 1)
                pe.wait_ge(k_copied, min(g + 2, G) if isinstance(g, int) else g + 2)
                if not (isinstance(g, int) and g == 0):
                    pe.wait_ge(scaled, 2 * g)
                if not (isinstance(g, int) and g == 0):
                    pe.wait_ge(token_ready, g)
                for j in range(2):
                    ins = nc.tensor.matmul(token_p[:, j * E:(j + 1) * E], logit_t[:, j * B:(j + 1) * B],
                                           fold_sb[:, :], start=True, stop=True)
                ins.then_inc(token_mm, 1)

            def weights(g):
                pe.wait_ge(weights_ready, g + 1)
                if not (isinstance(g, int) and g == 0):
                    pe.wait_ge(weight_t_ready, g)
                for j in range(2):
                    ins = nc.tensor.transpose(weight_p[:, j * B:(j + 1) * B],
                                              weight2[:, j, :, :].rearrange("p t e -> p (t e)"), ident[:, :])
                ins.then_inc(weight_mm, 1)

            def weight_sums(g):
                pe.wait_ge(token_ready, g + 1)
                pe.wait_ge(k_copied, min(g + 4, G) if isinstance(g, int) else g + 4)
                pe.wait_ge(weight_t_ready, g + 1)
                nc.tensor.matmul(wsum_p, ones[:, :], weight_t[:, :], start=True, stop=True)\
                  .then_inc(wsum_mm, 1)

            def bias(g, half):
                if not (isinstance(g, int) and g == 0 and half == 0):
                    pe.wait_ge(mixed, 2 * g + half)
                for q in range(2):
                    for odd in range(2):
                        cols = bass.ts(4 * half + 2 * q + odd, P)
                        nc.tensor.matmul(bias_p[:, odd, q, :], ebt_hi[:, cols], weight_t[:, :],
                                         start=True, stop=False)
                        ins = nc.tensor.matmul(bias_p[:, odd, q, :], ebt_lo[:, cols], weight_t[:, :],
                                               start=False, stop=True)
                ins.then_inc(bias_mm, 1)

            filters_of(0, 0, 0)
            filters_of(1, 0, 1)
            pe.wait_ge(consts_loaded, 112)
            pe.wait_ge(zeros_made, 2)
            pe.wait_ge(expert_lo_ready, 1)

            def group(g, it, k):
                if there(g):
                    convolve(g, it, k, 0, 0)
                if there(g - 2):
                    weight_sums(g - 2)
                if there(g - 1):
                    logits(g - 1, k - 1)
                if there(g - 2):
                    bias(g - 2, 0)
                if there(g):
                    convolve(g, it, k, 0, 1)
                if there(g - 1):
                    tokens(g - 1)
                if there(g - 2):
                    bias(g - 2, 1)
                if there(g):
                    convolve(g, it, k, 1, 0)
                if there(g + 2):
                    filters_of(g + 2, it, k + 2)
                if there(g):
                    convolve(g, it, k, 1, 1)
                if there(g - 1):
                    weights(g - 1)

            run(pe, group, G + 2)


def kernel(x, itok_B_78_3631, L0_cond_log_dt, L0_cond_C, L0_cond_log_A_real, L0_cond_A_imag, L0_cond_D,
           L0_ffn_router_weight, L0_ffn_router_bias, L0_ffn_expert_bias):
    import concourse.bacc as bacc
    from concourse.bass_utils import run_bass_kernel_spmd

    f32 = np.float32
    x, length = np.asarray(x), np.asarray(itok_B_78_3631)
    log_dt, c_in = np.asarray(L0_cond_log_dt), np.asarray(L0_cond_C)
    log_a, a_im, d = np.asarray(L0_cond_log_A_real), np.asarray(L0_cond_A_imag), np.asarray(L0_cond_D)
    rw, rb, eb = (np.asarray(a) for a in (L0_ffn_router_weight, L0_ffn_router_bias, L0_ffn_expert_bias))

    def twice(a):
        return np.concatenate([a.T, a.T], axis=0)

    modes = np.stack([np.broadcast_to(log_dt, (P, H)), twice(log_a), twice(a_im), twice(c_in[:, :, 0]),
                      twice(c_in[:, :, 1])], axis=1)
    steps = np.concatenate([np.arange(NI), NI * np.arange(NA), NI * np.arange(NA)])
    cosine_first = np.repeat([0.25, 0.0], N)[:, None]
    offsets = np.concatenate([np.broadcast_to(cosine_first, (P, NI + NA)),
                              np.broadcast_to(0.25 - cosine_first, (P, NA))], axis=1)
    by_group = x.reshape(B, G, 2, NC, P).transpose(1, 4, 3, 2, 0)
    sent = {
        "x": by_group.reshape(G, P, 2 * L),
        "x_rev": by_group[:, ::-1].reshape(G, P, 2 * L),
        "lens": np.broadcast_to(length, (P, B)),
        "modes": modes,
        "d_skip": d.reshape(1, H),
        "router": rw.reshape(E, NC, P).transpose(2, 1, 0),
        "router_bias": np.concatenate([rb, np.zeros(E, rb.dtype)]).reshape(P, 1),
        "expert_bias": np.concatenate([eb, eb], axis=0),
        "steps": np.broadcast_to(steps, (P, NJ)).astype(f32),
        "offsets": offsets.astype(f32),
        "l_index": (np.arange(P)[:, None] + P * np.arange(NC)[None, :]).astype(f32),
        "identity": np.eye(P, dtype=f32),
        "fold": np.concatenate([np.eye(E, dtype=f32)] * 2, axis=0),
    }
    sent = {name: np.ascontiguousarray(a) for name, a in sent.items()}

    nc = bacc.Bacc("TRN2", target_bir_lowering=False, num_devices=1)
    aps = {name: nc.dram_tensor(f"in_{name}", a.shape, mybir.dt.from_np(a.dtype), kind="ExternalInput").ap()
           for name, a in sent.items()}
    out = nc.dram_tensor("out_dram", (G, P, 2 * L), F32, kind="ExternalOutput").ap()
    build(nc, out=out, **aps)
    result = run_bass_kernel_spmd(nc, [{f"in_{name}": a for name, a in sent.items()}], core_ids=[0])
    got = result.results[0]["out_dram"]
    return got.reshape(G, P, NC, 2, B).transpose(4, 0, 3, 2, 1).reshape(B, H, L)
```

```python
from contextlib import ExitStack

import numpy as np

import concourse.bass as bass
from concourse import mybir

F32 = mybir.dt.float32
F32R = mybir.dt.float32r
I32 = mybir.dt.int32
ALU = mybir.AluOpType
ACT = mybir.ActivationFunctionType

P = 128
B, H, L = 128, 64, 1024
N, E, TOP = 64, 64, 8
NC = L // P
HALF = NC // 2
G = H // 2
UNROLL = 4
HB = 2 * UNROLL
NI, NA = 64, L // 64
NJ = NI + 2 * NA
ROW = P + L

ROUND = 1.5 * 2.0 ** 23
ROUND18 = 1.5 * 2.0 ** 5
TWO_PI = 6.283184
LOWEST = -3.4028235e38
LN2_HI, LN2_LO = 0.693359375, -2.12194440e-4
LOG2_E = 1.4426950408889634
EXP_SERIES = (1.0 / 5040, 1.0 / 720, 1.0 / 120, 1.0 / 24, 1.0 / 6, 0.5, 1.0)


def inverse_two_pi_parts():
    x = 1.0 / (2.0 * np.pi)
    c1 = np.round(x * 2 ** 14) / 2 ** 14
    c2 = np.round((x - c1) * 2 ** 26) / 2 ** 26
    return float(c1), float(c2), float(x - c1 - c2)


def build(nc, x, x_rev, lens, modes, d_skip, router, router_bias, expert_bias, steps, offsets, l_index,
          identity, out):
    ctx = ExitStack()
    with ctx:
        def sb(name, shape, dt=F32):
            return ctx.enter_context(nc.sbuf_tensor(name, shape, dt))

        def ps(name, shape):
            return ctx.enter_context(nc.psum_tensor(name, shape, F32))

        def sem(name):
            return ctx.enter_context(nc.semaphore(name))

        filters = nc.dram_tensor("filters", [H, ROW], F32, kind="Internal").ap()
        toeplitz = bass.AP(filters.tensor, filters.offset + 1, [[ROW, H], [1, P], [1, L]])

        xs = [sb(f"xs{i}", [P, NC, 2, B]) for i in range(2)]
        us = [sb(f"us{i}", [P, NC, 2, B]) for i in range(2)]
        u_hi = [sb(f"u_hi{i}", [P, NC, 2, B], F32R) for i in range(2)]
        u_lo = [sb(f"u_lo{i}", [P, NC, 2, B], F32R) for i in range(2)]
        toe = [sb(f"toe{i}", [P, L]) for i in range(4)]
        toe_hi = [sb(f"toe_hi{i}", [P, L], F32R) for i in range(2)]
        toe_lo = [sb(f"toe_lo{i}", [P, L], F32R) for i in range(2)]
        zs = [sb(f"zs{i}", [P, NC, 2, B]) for i in range(4)]
        mask = sb("mask", [P, NC, B])
        len_i = sb("len_i", [P, B], I32)
        len_f = sb("len_f", [P, B])
        l_idx = sb("l_idx", [P, NC])
        rwt = sb("rwt", [P, NC, E])
        rbias = sb("rbias", [P, 1])
        ebt = sb("ebt", [P, L])
        ebt_hi = sb("ebt_hi", [P, L], F32R)
        ebt_lo = sb("ebt_lo", [P, L], F32R)
        ident = sb("ident", [P, P])
        ones = sb("ones", [P, P], F32R)
        logit_t = sb("logit_t", [P, 2 * B])
        halves = sb("halves", [P, 2, 2, E])
        token = sb("token", [P, 2, E])
        top8 = sb("top8", [P, 2, TOP])
        neg_max = sb("neg_max", [P, 2])
        escore = sb("escore", [P, 2, E])
        esum = sb("esum", [P, 2])
        rsum = sb("rsum", [P, 2])
        dropped = sb("dropped", [P, 2, E])
        kept = sb("kept", [P, 2, E])
        weight2 = sb("weight2", [P, 2, 2, E])
        weight_t = sb("weight_t", [P, 2 * B], F32R)
        md = sb("md", [P, 5, H])
        dsk = sb("dsk", [1, H])
        st = sb("st", [P, NJ])
        off = sb("off", [P, NJ])
        cx = sb("cx", [P, 24, H])
        qx = sb("qx", [P, 6, H])
        cb_hi = sb("cb_hi", [P, H], F32R)
        ci = sb("ci", [P, 2, H], I32)
        turn_hi = sb("turn_hi", [P, H])
        turn_lo = sb("turn_lo", [P, H])
        decay = sb("decay", [P, H])
        coef_own = sb("coef_own", [P, H])
        coef_oth = sb("coef_oth", [P, H])
        ph = sb("ph", [P, HB, NJ])
        ph_int = sb("ph_int", [P, HB, NJ])
        ph_lo = sb("ph_lo", [P, HB, NJ])
        dec = sb("dec", [P, HB, NI + NA])
        sn = sb("sn", [P, HB, NJ])
        ex = sb("ex", [P, HB, NI + NA])
        w_own = sb("w_own", [P, HB, NA])
        w_oth = sb("w_oth", [P, HB, NA])
        tab_v = sb("tab_v", [P, HB, NI])
        tab_w = sb("tab_w", [P, HB, NA])
        k_sb = sb("k_sb", [NA, 2, NI])
        zeros = sb("zeros", [H, P])

        y = [ps(f"y{i}", [P, NC, B]) for i in range(2)]
        bank_t = ps("bank_t", [P, 512])
        bank_s = ps("bank_s", [P, 512])
        bias_p = ps("bias_p", [P, 2, 2, 2 * B])
        logit_p = bank_t[:, 0:256]
        weight_p = bank_t[:, 256:512]
        token_p = bank_t[:, 0:256]
        wsum_p = bank_s[:, 0:256]
        filter_p = bank_s[0:NA, 256:384]

        x_loaded = [sem(f"x_loaded{i}") for i in range(2)]
        u_loaded = [sem(f"u_loaded{i}") for i in range(2)]
        first_loaded = sem("first_loaded")
        first_hi_ready = sem("first_hi_ready")
        first_lo_ready = sem("first_lo_ready")
        toe_loaded = [sem(f"toe_loaded{i}") for i in range(4)]
        out_stored = [sem(f"out_stored{i}") for i in range(4)]
        modes_loaded = sem("modes_loaded")
        steps_loaded = sem("steps_loaded")
        consts_loaded = sem("consts_loaded")
        zeros_made = sem("zeros_made")
        pad_written = sem("pad_written")
        filter_written = sem("filter_written")
        const_step = sem("const_step")
        const_hi = sem("const_hi")
        mask_ready = sem("mask_ready")
        quotient_step = sem("quotient_step")
        exps_ready = sem("exps_ready")
        turns_ready = sem("turns_ready")
        head_pool = sem("head_pool")
        head_dve = sem("head_dve")
        head_act = sem("head_act")
        tab_pool = sem("tab_pool")
        tab_dve = sem("tab_dve")
        tab_act = sem("tab_act")
        filter_mm = sem("filter_mm")
        k_copied = sem("k_copied")
        k_full = sem("k_full")
        toe_hi_ready = sem("toe_hi_ready")
        toe_lo_ready = sem("toe_lo_ready")
        u_hi_ready = sem("u_hi_ready")
        u_lo_ready = sem("u_lo_ready")
        conv_half = sem("conv_half")
        z_half = sem("z_half")
        logits_mm = sem("logits_mm")
        logit_t_ready = sem("logit_t_ready")
        token_mm = sem("token_mm")
        halves_ready = sem("halves_ready")
        token_ready = sem("token_ready")
        max_step = sem("max_step")
        exp_done = sem("exp_done")
        drop_done = sem("drop_done")
        kept_step = sem("kept_step")
        weights_ready = sem("weights_ready")
        weight_mm = sem("weight_mm")
        weight_hi_ready = sem("weight_hi_ready")
        weight_t_ready = sem("weight_t_ready")
        expert_hi_ready = sem("expert_hi_ready")
        expert_lo_ready = sem("expert_lo_ready")
        wsum_mm = sem("wsum_mm")
        bias_mm = sem("bias_mm")
        scaled = sem("scaled")
        mixed = sem("mixed")
        final = sem("final")
        last_final = sem("last_final")

        block = ctx.enter_context(nc.Block())

        def run(eng, group, last):
            for g in range(UNROLL):
                group(g, 0, g)
            with eng.Fori(1, G // UNROLL - 1, 1) as it:
                for k in range(UNROLL):
                    group(it * UNROLL + k, it, k)
            for g in range(G - UNROLL, last):
                group(g, g // UNROLL, g % UNROLL)

        def bias_in(g, half):
            if isinstance(g, int) and g >= G - 2 and half == 1:
                return y[g % 2][:, :, :].rearrange("p (t q j) b -> p t q (j b)", t=2, q=2)
            return bias_p[:, :, :, :]

        def there(g):
            return 0 <= g < G if isinstance(g, int) else True

        @block.sync
        def _(sp):
            sp.dma_start(md[:, :, :], modes).then_inc(modes_loaded, 16)
            sp.dma_start(us[0][:, :, :, :], x_rev[0]).then_inc(u_loaded[0], 16)
            sp.dma_start(st[:, :], steps).then_inc(steps_loaded, 16)
            sp.dma_start(off[:, :], offsets).then_inc(steps_loaded, 16)
            sp.dma_start(dsk[:, :], d_skip).then_inc(steps_loaded, 16)
            sp.dma_start(len_i[:, :], lens).then_inc(consts_loaded, 16)
            sp.dma_start(l_idx[:, :], l_index).then_inc(consts_loaded, 16)
            sp.dma_start(rwt[:, :, :], router).then_inc(consts_loaded, 16)
            sp.dma_start(rbias[:, :], router_bias).then_inc(consts_loaded, 16)
            sp.dma_start(ebt[:, :], expert_bias).then_inc(consts_loaded, 16)
            sp.dma_start(ident[:, :], identity).then_inc(consts_loaded, 16)
            sp.dma_start(us[1][:, :, :, :], x_rev[1]).then_inc(u_loaded[1], 16)
            sp.wait_ge(zeros_made, 1)
            sp.dma_start(filters[:, 0:P], zeros[:, :]).then_inc(pad_written, 16)

            def write_filter(g):
                sp.wait_ge(k_full, g + 1)
                sp.dma_start(filters[bass.ts(g, 2), P:ROW].rearrange("s (a i) -> a s i", a=NA), k_sb[:, :, :])\
                  .then_inc(filter_written, 16)

            def load_toeplitz(g, k):
                for j in range(2):
                    slot = (2 * k + j) % 4
                    if not (isinstance(g, int) and g < 2):
                        sp.wait_ge(toe_lo_ready, 2 * g + j - 3)
                    if j == 0:
                        sp.wait_ge(filter_written, 16 * g + 16)
                    sp.dma_start(toe[slot][:, :], toeplitz[2 * g + j]).then_inc(toe_loaded[slot], 16)

            sp.wait_ge(pad_written, 16)
            write_filter(0)
            sp.wait_ge(filter_written, 16)
            for half in range(2):
                cols = slice(half * L // 2, (half + 1) * L // 2)
                sp.dma_start(toe[0][:, cols], toeplitz[0][:, cols])\
                  .then_inc(toe_loaded[0] if half else first_loaded, 16)
            sp.dma_start(toe[1][:, :], toeplitz[1]).then_inc(toe_loaded[1], 16)
            write_filter(1)

            def group(g, it, k):
                if there(g + 2):
                    sp.wait_ge(u_lo_ready, g + 1)
                    sp.dma_start(us[k % 2][:, :, :, :], x_rev[g + 2]).then_inc(u_loaded[k % 2], 16)
                if there(g + 1):
                    load_toeplitz(g + 1, k + 1)
                if there(g - 2):
                    for half in range(2):
                        if half == 1 and not there(g - 1):
                            sp.wait_ge(last_final, 1)
                        else:
                            sp.wait_ge(final, 2 * g - 3 + half)
                        cs = slice(half * HALF, (half + 1) * HALF)
                        sp.dma_start(out[g - 2].rearrange("p (c n) -> p c n", c=NC)[:, cs, :],
                                     zs[(k - 2) % 4][:, cs, :, :].rearrange("p c j b -> p c (j b)"))\
                          .then_inc(out_stored[(k - 2) % 4], 16)
                if there(g):
                    sp.dma_start(xs[k % 2][:, :, :, :], x[g]).then_inc(x_loaded[k % 2], 16)
                if there(g + 2):
                    write_filter(g + 2)

            run(sp, group, G + 2)
            for i in range(4):
                sp.wait_ge(out_stored[i], 32 * (G // 4))

        @block.gpsimd
        def _(pool):
            nc.gpsimd.memset(zeros[:, :], 0.0).then_inc(zeros_made, 1)
            nc.gpsimd.memset(ones[:, :].bitcast(F32), 1.0).then_inc(zeros_made, 1)

            def tables(nb, c0=0, c1=HB, done=tab_pool):
                n = c1 - c0
                hs = slice(c0, c1) if isinstance(nb, int) and nb == 0 else bass.ts(nb, HB)
                if not (isinstance(nb, int) and nb == 0):
                    pool.wait_ge(tab_dve, 10 * nb)

                def along_steps(a, width=NJ):
                    return a[:, hs].unsqueeze(2).broadcast_to([P, n, width])

                def for_channels(a, width=NJ):
                    return a[:, 0:width].unsqueeze(1).broadcast_to([P, n, width])

                nc.gpsimd.tensor_tensor(ph[:, c0:c1, :], along_steps(turn_hi), for_channels(st), ALU.mult)\
                  .then_inc(done, 1)
                nc.gpsimd.tensor_tensor(ph_lo[:, c0:c1, :], along_steps(turn_lo), for_channels(st), ALU.mult)\
                  .then_inc(done, 1)
                pool.wait_ge(done, 4 * nb + 1)
                nc.gpsimd.tensor_tensor(ph[:, c0:c1, :], ph[:, c0:c1, :], for_channels(off), ALU.add)\
                  .then_inc(done, 1)
                nc.gpsimd.tensor_tensor(dec[:, c0:c1, :], along_steps(decay, NI + NA), for_channels(st, NI + NA),
                                        ALU.mult).then_inc(done, 1)

            def residual(g, it, k, half):
                cs = slice(half * HALF, (half + 1) * HALF)
                pool.wait_ge(x_loaded[k % 2], 32 * it + 16 * (k // 2) + 16)
                pool.wait_ge(mixed, 2 * g + half + 1)
                nc.gpsimd.tensor_tensor(zs[k % 4][:, cs, :, :], zs[k % 4][:, cs, :, :], xs[k % 2][:, cs, :, :],
                                        ALU.add).then_inc(final, 1)

            def split_toeplitz(g, k, j):
                pool.wait_ge(toe_hi_ready, 2 * g + j + 1)
                nc.gpsimd.tensor_tensor(toe_lo[j][:, :], toe[(2 * k + j) % 4][:, :], toe_hi[j][:, :].bitcast(F32),
                                        ALU.subtract).then_inc(toe_lo_ready, 1)

            def step(n, o, a, b, op):
                if n:
                    pool.wait_ge(quotient_step, n)
                nc.gpsimd.tensor_tensor(o, a, b, op).then_inc(quotient_step, 1)

            pool.wait_ge(modes_loaded, 16)
            pool.wait_ge(exps_ready, 1)
            are, aim, c_re, c_im = cx[:, 13, :], md[:, 2, :], md[:, 3, :], md[:, 4, :]
            q = [qx[:, i, :] for i in range(6)]
            step(0, q[0], are, are, ALU.mult)
            step(1, q[1], aim, aim, ALU.mult)
            step(2, q[0], q[0], q[1], ALU.add)
            step(3, q[2], c_im, aim, ALU.mult)
            step(4, q[3], c_re, are, ALU.mult)
            step(5, q[2], q[2], q[3], ALU.subtract)
            step(6, q[4], c_im, are, ALU.mult)
            step(7, q[5], c_re, aim, ALU.mult)
            step(8, q[4], q[4], q[5], ALU.add)
            pool.wait_ge(turns_ready, 1)
            pool.wait_ge(steps_loaded, 48)
            tables(0, 0, 2, head_pool)
            tables(0, 2, HB)
            pool.wait_ge(u_hi_ready, 1)
            nc.gpsimd.tensor_tensor(u_lo[0][:, :, :, :], us[0][:, :, :, :], u_hi[0][:, :, :, :].bitcast(F32),
                                    ALU.subtract).then_inc(u_lo_ready, 1)
            pool.wait_ge(toe_lo_ready, 1)

            def group(g, it, k):
                if there(g):
                    split_toeplitz(g, k, 1)
                if there(g - 2):
                    residual(g - 2, it, k - 2, 0)
                if there(g + 1):
                    split_toeplitz(g + 1, k + 1, 0)
                if there(g - 2) and there(g - 1):
                    residual(g - 2, it, k - 2, 1)
                if k == 0 and there(g + UNROLL):
                    tables(it + 1)

            run(pool, group, G + 2)

        @block.scalar
        def _(act):
            def split(g, it, k):
                act.wait_ge(u_loaded[k % 2], 32 * it + 16 * (k // 2) + 16)
                if not (isinstance(g, int) and g < 2):
                    act.wait_ge(conv_half, 4 * g - 4)
                nc.scalar.activation(u_hi[k % 2][:, :, :, :], us[k % 2][:, :, :, :], ACT.Copy)\
                  .then_inc(u_hi_ready, 1)

            def tables(nb, c0=0, c1=HB):
                act.wait_ge(tab_dve, 10 * nb + 5)
                nc.scalar.activation(sn[:, c0:c1, :], ph[:, c0:c1, :], ACT.Sin, scale=TWO_PI).then_inc(tab_act, 1)
                act.wait_ge(tab_pool, 4 * nb + 4)
                nc.scalar.activation(ex[:, c0:c1, :], dec[:, c0:c1, :], ACT.Exp).then_inc(tab_act, 1)

            def take_filter(g):
                if not (isinstance(g, int) and g == 0):
                    act.wait_ge(filter_written, 16 * g)
                act.wait_ge(filter_mm, g + 1)
                nc.scalar.activation(k_sb[:, :, :].rearrange("a j i -> a (j i)"), filter_p, ACT.Copy)\
                  .then_inc(k_copied, 1)

            def split_toeplitz(g, it, k, j):
                slot = (2 * k + j) % 4
                act.wait_ge(toe_loaded[slot], 32 * it + 16 * ((2 * k + j) // 4) + 16)
                if not (isinstance(g, int) and g == 0):
                    act.wait_ge(conv_half, 4 * g + 2 * j - 2)
                nc.scalar.activation(toe_hi[j][:, :], toe[slot][:, :], ACT.Copy).then_inc(toe_hi_ready, 1)

            act.wait_ge(const_hi, 1)
            nc.scalar.activation(cb_hi[:, :], cx[:, 0, :], ACT.Copy).then_inc(const_hi, 1)
            split(0, 0, 0)
            act.wait_ge(const_hi, 3)
            nc.scalar.activation(cx[:, 10, :], cx[:, 9, :], ACT.Sin, scale=TWO_PI).then_inc(const_hi, 1)
            nc.scalar.activation(cx[:, 11, :], cx[:, 9, :], ACT.Sin, scale=TWO_PI / 2).then_inc(const_hi, 1)
            act.wait_ge(head_pool, 4)
            nc.scalar.activation(ex[:, 0:2, :], dec[:, 0:2, :], ACT.Exp).then_inc(head_act, 1)
            act.wait_ge(head_dve, 5)
            nc.scalar.activation(sn[:, 0:2, :], ph[:, 0:2, :], ACT.Sin, scale=TWO_PI).then_inc(head_act, 1)
            take_filter(0)
            tables(0, 2)
            act.wait_ge(consts_loaded, 96)
            nc.scalar.activation(ebt_hi[:, :], ebt[:, :], ACT.Copy).then_inc(expert_hi_ready, 1)
            for half in range(2):
                cols = slice(half * L // 2, (half + 1) * L // 2)
                act.wait_ge(toe_loaded[0] if half else first_loaded, 16)
                nc.scalar.activation(toe_hi[0][:, cols], toe[0][:, cols], ACT.Copy).then_inc(first_hi_ready, 1)
            act.wait_ge(first_hi_ready, 2)
            act.sem_inc(toe_hi_ready, 1)
            take_filter(1)

            def group(g, it, k):
                if there(g - 2):
                    act.wait_ge(weight_mm, g - 1)
                    if not (isinstance(g, int) and g == 2):
                        act.wait_ge(bias_mm, 2 * (g - 2))
                    nc.scalar.activation(weight_t[:, :], weight_p, ACT.Copy).then_inc(weight_hi_ready, 1)
                if there(g):
                    split_toeplitz(g, it, k, 1)
                if there(g - 1):
                    act.wait_ge(logits_mm, g)
                    nc.scalar.activation(logit_t[:, :], logit_p, ACT.Identity, bias=rbias[:, 0:1])\
                      .then_inc(logit_t_ready, 1)
                if there(g + 1):
                    split(g + 1, it, k + 1)
                if k == 2 and there(g + UNROLL - k):
                    tables(it + 1)
                if there(g - 1):
                    act.wait_ge(token_mm, g)
                    if not (isinstance(g, int) and g == 1):
                        act.wait_ge(token_ready, g - 1)
                    nc.scalar.activation(halves[:, :, :, :].rearrange("p j t e -> p (j t e)"), token_p, ACT.Copy)\
                      .then_inc(halves_ready, 1)
                if there(g + 1):
                    split_toeplitz(g + 1, it, k + 1, 0)
                if there(g - 1):
                    act.wait_ge(max_step, 3 * g)
                    for j in range(2):
                        ins = nc.scalar.activation(escore[:, j, :], token[:, j, :], ACT.Exp,
                                                   bias=neg_max[:, j:j + 1], accum_out=esum[:, j:j + 1])
                    ins.then_inc(exp_done, 1)
                if there(g + 2):
                    take_filter(g + 2)

            run(act, group, G + 2)

        @block.vector
        def _(dve):
            steps_done = [0]

            def link(ins, behind=0):
                steps_done[0] += 1
                ins.then_inc(const_step, 1)
                dve.wait_ge(const_step, steps_done[0] - behind)

            def tt(o, a, b, op, behind=0):
                link(nc.vector.tensor_tensor(o, a, b, op), behind)

            def ts(o, a, s1, s2, op0, op1, behind=0):
                link(nc.vector.tensor_scalar(o, a, s1, s2, op0, op1), behind)

            def stt(o, a, s, b, op0, op1, behind=0):
                link(nc.vector.scalar_tensor_tensor(o, a, s, b, op0, op1), behind)

            steady = (tab_pool, tab_dve, tab_act)
            head = (head_pool, head_dve, head_act)

            def reduce_phases(nb, c0, c1, from_pool, done, from_act, steps):
                t, whole, low = (a[:, c0:c1, :] for a in (ph, ph_int, ph_lo))
                for n in steps:
                    if n == 0:
                        dve.wait_ge(from_pool, 4 * nb + 3)
                    else:
                        dve.wait_ge(done, 10 * nb + n)
                    if n in (0, 3):
                        ins = nc.vector.tensor_scalar(whole, t, ROUND, ROUND, ALU.add, ALU.subtract)
                    elif n in (1, 4):
                        ins = nc.vector.tensor_tensor(t, t, whole, ALU.subtract)
                    else:
                        ins = nc.vector.tensor_tensor(t, t, low, ALU.add)
                    ins.then_inc(done, 1)

            def make_tables(nb, c0, c1, from_pool, done, from_act):
                n = c1 - c0
                hs = slice(c0, c1) if isinstance(nb, int) and nb == 0 else bass.ts(nb, HB)
                dve.wait_ge(from_act, 2 * nb + 2)
                if not (isinstance(nb, int) and nb == 0):
                    dve.wait_ge(filter_mm, UNROLL * nb)
                nc.vector.tensor_tensor(tab_v[:, c0:c1, :], sn[:, c0:c1, 0:NI], ex[:, c0:c1, 0:NI], ALU.mult)\
                  .then_inc(done, 1)
                nc.vector.tensor_tensor(w_own[:, c0:c1, :], sn[:, c0:c1, NI:NI + NA],
                                        coef_own[:, hs].unsqueeze(2).broadcast_to([P, n, NA]), ALU.mult)\
                  .then_inc(done, 1)
                nc.vector.tensor_tensor(w_oth[:, c0:c1, :], sn[:, c0:c1, NI + NA:NJ],
                                        coef_oth[:, hs].unsqueeze(2).broadcast_to([P, n, NA]), ALU.mult)\
                  .then_inc(done, 1)
                dve.wait_ge(done, 10 * nb + 8)
                nc.vector.tensor_tensor(w_own[:, c0:c1, :], w_own[:, c0:c1, :], w_oth[:, c0:c1, :], ALU.add)\
                  .then_inc(done, 1)
                dve.wait_ge(done, 10 * nb + 9)
                nc.vector.tensor_tensor(tab_w[:, c0:c1, :], w_own[:, c0:c1, :], ex[:, c0:c1, NI:NI + NA], ALU.mult)\
                  .then_inc(done, 1)

            c = [cx[:, i, :] for i in range(24)]
            dve.wait_ge(modes_loaded, 16)
            both = ((md[:, 0, :], c[14], c[16], c[18], 0), (md[:, 1, :], c[15], c[17], c[19], 1))
            for x_in, k, _, _, _ in both:
                ts(k, x_in, LOG2_E, ROUND, ALU.mult, ALU.add, behind=1)
            for _, k, _, _, _ in both:
                ts(k, k, ROUND, None, ALU.subtract, ALU.bypass, behind=1)
            for _, k, _, _, _ in both:
                ts(k, k, -126.0, 127.0, ALU.max, ALU.min, behind=1)
            for x_in, k, rest, _, _ in both:
                stt(rest, k, -LN2_HI, x_in, ALU.mult, ALU.add, behind=1)
            for _, k, rest, _, _ in both:
                stt(rest, k, -LN2_LO, rest, ALU.mult, ALU.add, behind=1)
            for _, _, rest, q, _ in both:
                ts(q, rest, EXP_SERIES[0], None, ALU.mult, ALU.bypass, behind=1)
            for term in EXP_SERIES[1:]:
                for _, _, rest, q, _ in both:
                    stt(q, q, term, rest, ALU.add, ALU.mult, behind=1)
            for _, k, _, _, j in both:
                ts(ci[:, j, :], k, 127.0, 2.0 ** 23, ALU.add, ALU.mult, behind=1)
            for _, _, _, q, j in both:
                stt(cx[:, 12 + j, :], q, 1.0, ci[:, j, :].bitcast(F32), ALU.add, ALU.mult, behind=1)
            dve.wait_ge(const_step, steps_done[0])
            dt, are, aim = cx[:, 12, :], cx[:, 13, :], md[:, 2, :]
            dve.sem_inc(exps_ready, 1)
            tt(c[0], aim, dt, ALU.mult)
            dve.sem_inc(const_hi, 1)
            stt(decay[:, :], are, -1.0, dt, ALU.mult, ALU.mult)
            c1, c2, c3 = inverse_two_pi_parts()
            bh = cb_hi[:, :].bitcast(F32)
            k, rest, q, two_k = c[14], c[15], c[16], ci[:, 0, :].bitcast(F32)
            ts(k, decay[:, :], LOG2_E, ROUND, ALU.mult, ALU.add)
            ts(k, k, ROUND, None, ALU.subtract, ALU.bypass)
            dve.wait_ge(const_hi, 2)
            tt(c[1], c[0], bh, ALU.subtract, behind=1)
            ts(k, k, -126.0, 127.0, ALU.max, ALU.min, behind=1)
            ts(c[2], bh, c1, None, ALU.mult, ALU.bypass, behind=1)
            stt(rest, k, -LN2_HI, decay[:, :], ALU.mult, ALU.add, behind=1)
            ts(c[3], c[2], ROUND, ROUND, ALU.add, ALU.subtract, behind=1)
            stt(rest, k, -LN2_LO, rest, ALU.mult, ALU.add, behind=1)
            tt(c[2], c[2], c[3], ALU.subtract, behind=1)
            ts(ci[:, 0, :], k, 127.0, 2.0 ** 23, ALU.add, ALU.mult, behind=1)
            ts(c[4], c[1], c1, None, ALU.mult, ALU.bypass, behind=1)
            ts(q, rest, EXP_SERIES[0], None, ALU.mult, ALU.bypass, behind=1)
            tt(c[3], c[2], c[4], ALU.add, behind=1)
            stt(q, q, EXP_SERIES[1], rest, ALU.add, ALU.mult, behind=1)
            ts(c[5], bh, c2, None, ALU.mult, ALU.bypass)
            tt(c[3], c[3], c[5], ALU.add, behind=1)
            stt(q, q, EXP_SERIES[2], rest, ALU.add, ALU.mult, behind=1)
            ts(turn_hi[:, :], c[3], ROUND18, ROUND18, ALU.add, ALU.subtract, behind=1)
            stt(q, q, EXP_SERIES[3], rest, ALU.add, ALU.mult, behind=1)
            tt(c[2], c[2], turn_hi[:, :], ALU.subtract, behind=1)
            stt(q, q, EXP_SERIES[4], rest, ALU.add, ALU.mult, behind=1)
            tt(c[2], c[2], c[4], ALU.add, behind=1)
            stt(q, q, EXP_SERIES[5], rest, ALU.add, ALU.mult, behind=1)
            tt(c[2], c[2], c[5], ALU.add, behind=1)
            stt(q, q, EXP_SERIES[6], rest, ALU.add, ALU.mult, behind=1)
            stt(c[2], bh, c3, c[2], ALU.mult, ALU.add, behind=1)
            tt(c[18], q, two_k, ALU.mult, behind=1)
            stt(turn_lo[:, :], c[1], c2, c[2], ALU.mult, ALU.add, behind=1)
            stt(c[17], q, 1.0, two_k, ALU.add, ALU.mult)
            dve.sem_inc(turns_ready, 1)
            tt(c[8], turn_hi[:, :], turn_lo[:, :], ALU.add, behind=1)
            stt(c[18], two_k, -1.0, c[18], ALU.add, ALU.add, behind=1)
            ts(c[7], c[8], ROUND, ROUND, ALU.add, ALU.subtract)
            tt(c[9], c[8], c[7], ALU.subtract)
            dve.sem_inc(const_hi, 1)
            dve.wait_ge(quotient_step, 9)
            link(nc.vector.reciprocal(c[22], qx[:, 0, :]))
            stt(c[23], qx[:, 2, :], 2.0, c[22], ALU.mult, ALU.mult, behind=1)
            stt(c[6], qx[:, 4, :], 2.0, c[22], ALU.mult, ALU.mult, behind=1)
            reduce_phases(0, 0, 2, *head, steps=(0,))
            dve.wait_ge(const_hi, 5)
            stt(c[19], c[11], -2.0, c[11], ALU.mult, ALU.mult, behind=1)
            tt(c[21], c[17], c[10], ALU.mult, behind=1)
            reduce_phases(0, 0, 2, *head, steps=(1,))
            tt(c[20], c[19], c[17], ALU.mult, behind=1)
            reduce_phases(0, 0, 2, *head, steps=(2,))
            tt(c[5], c[6], c[21], ALU.mult, behind=1)
            reduce_phases(0, 0, 2, *head, steps=(3,))
            tt(c[20], c[20], c[18], ALU.add, behind=1)
            reduce_phases(0, 0, 2, *head, steps=(4,))
            tt(c[7], c[23], c[21], ALU.mult, behind=1)
            tt(c[3], c[23], c[20], ALU.mult, behind=1)
            tt(c[8], c[6], c[20], ALU.mult, behind=1)
            tt(coef_own[0:N, :], cx[0:N, 3, :], cx[0:N, 5, :], ALU.add, behind=1)
            stt(coef_own[N:P, :], cx[N:P, 3, :], -1.0, cx[N:P, 5, :], ALU.mult, ALU.subtract, behind=1)
            tt(coef_oth[:, :], c[8], c[7], ALU.subtract)

            def add_skip(g):
                dve.wait_ge(k_copied, g + 1)
                nc.vector.tensor_tensor(k_sb[0:1, :, 0], k_sb[0:1, :, 0], dsk[0:1, bass.ts(g, 2)], ALU.add)\
                  .then_inc(k_full, 1)

            def split(g, k):
                dve.wait_ge(u_hi_ready, g + 1)
                nc.vector.tensor_tensor(u_lo[k % 2][:, :, :, :], us[k % 2][:, :, :, :],
                                        u_hi[k % 2][:, :, :, :].bitcast(F32), ALU.subtract)\
                  .then_inc(u_lo_ready, 1)

            def masked(g, it, k, j, half):
                cs = slice(half * HALF, (half + 1) * HALF)
                if j == 0 and half == 0 and not (isinstance(g, int) and g < 4):
                    dve.wait_ge(out_stored[k], 32 * it)
                dve.wait_ge(conv_half, 4 * g + 2 * j + half + 1)
                nc.vector.tensor_tensor(zs[k][:, cs, j, :], y[j][:, cs, :], mask[:, cs, :], ALU.mult)\
                  .then_inc(z_half, 1)

            def add_logits(g):
                dve.wait_ge(halves_ready, g + 1)
                if not (isinstance(g, int) and g == 0):
                    dve.wait_ge(exp_done, g)
                nc.vector.tensor_tensor(token[:, :, :], halves[:, :, 0, :], halves[:, :, 1, :], ALU.add)\
                  .then_inc(token_ready, 1)

            def softmax(g):
                for j in range(2):
                    nc.vector.max(top8[:, j, :], token[:, j, :]).then_inc(max_step, 1)
                dve.wait_ge(max_step, 3 * g + 2)
                nc.vector.tensor_scalar(neg_max[:, :], top8[:, :, 0], -1.0, None, ALU.mult, ALU.bypass)\
                  .then_inc(max_step, 1)
                for j in range(2):
                    ins = nc.vector.match_replace(out=dropped[:, j, :], in_to_replace=top8[:, j, :],
                                                  in_values=token[:, j, :], imm_value=LOWEST)
                ins.then_inc(drop_done, 1)
                dve.wait_ge(exp_done, g + 1)
                nc.vector.reciprocal(rsum[:, :], esum[:, :]).then_inc(kept_step, 1)
                dve.wait_ge(drop_done, g + 1)
                nc.vector.scalar_tensor_tensor(kept[:, :, :], dropped[:, :, :], LOWEST, escore[:, :, :],
                                               ALU.is_equal, ALU.mult).then_inc(kept_step, 1)
                dve.wait_ge(kept_step, 2 * g + 2)
                if not (isinstance(g, int) and g == 0):
                    dve.wait_ge(weight_mm, g)
                nc.vector.tensor_tensor(weight2[:, :, :, :], kept[:, :, :].unsqueeze(2).broadcast_to([P, 2, 2, E]),
                                        rsum[:, :].unsqueeze(2).unsqueeze(3).broadcast_to([P, 2, 2, E]), ALU.mult)\
                  .then_inc(weights_ready, 1)

            def low_weights(g):
                dve.wait_ge(weight_hi_ready, g + 1)
                nc.vector.tensor_tensor(weight_t[E:P, :], weight_p[E:P, :], weight_t[E:P, :].bitcast(F32),
                                        ALU.subtract).then_inc(weight_t_ready, 1)

            def scale(g, k, half):
                dve.wait_ge(wsum_mm, g + 1)
                zv = zs[k % 4][:, half * HALF:(half + 1) * HALF, :, :].rearrange("p c j b -> p c (j b)")
                nc.vector.tensor_tensor(zv, zv, wsum_p.unsqueeze(1).broadcast_to([P, HALF, 2 * B]), ALU.mult)\
                  .then_inc(scaled, 1)

            def mix(g, k, half):
                cs = slice(half * HALF, (half + 1) * HALF)
                dve.wait_ge(scaled, 2 * g + half + 1)
                dve.wait_ge(bias_mm, 2 * g + half + 1)
                zv = zs[k % 4][:, cs, :, :].rearrange("p (q t) j b -> p q t (j b)", t=2)
                nc.vector.tensor_tensor(zv, zv, bias_in(g, half).rearrange("p t q n -> p q t n"), ALU.add)\
                  .then_inc(mixed, 1)

            def last_residual():
                cs = slice(HALF, NC)
                dve.wait_ge(x_loaded[(G - 1) % 2], 16 * (G // 2))
                dve.wait_ge(mixed, 2 * G)
                nc.vector.tensor_tensor(zs[(G - 1) % 4][:, cs, :, :], zs[(G - 1) % 4][:, cs, :, :],
                                        xs[(G - 1) % 2][:, cs, :, :], ALU.add).then_inc(last_final, 1)

            make_tables(0, 0, 2, *head)
            reduce_phases(0, 2, HB, *steady, steps=(0, 1))
            add_skip(0)
            reduce_phases(0, 2, HB, *steady, steps=(2, 3, 4))
            dve.wait_ge(consts_loaded, 96)
            nc.vector.tensor_copy(len_f[:, :], len_i[:, :]).then_inc(mask_ready, 1)
            dve.wait_ge(mask_ready, 1)
            for cc in range(NC):
                nc.vector.tensor_scalar(mask[:, cc, :], len_f[:, :], l_idx[:, cc:cc + 1], None, ALU.is_gt,
                                        ALU.bypass).then_inc(mask_ready, 1)
            make_tables(0, 2, HB, *steady)
            for half in range(2):
                cols = slice(half * L // 2, (half + 1) * L // 2)
                dve.wait_ge(first_hi_ready, half + 1)
                nc.vector.tensor_tensor(toe_lo[0][:, cols], toe[0][:, cols], toe_hi[0][:, cols].bitcast(F32),
                                        ALU.subtract).then_inc(first_lo_ready, 1)
            dve.wait_ge(first_lo_ready, 2)
            dve.sem_inc(toe_lo_ready, 1)
            dve.wait_ge(mask_ready, 1 + NC)
            dve.wait_ge(expert_hi_ready, 1)
            nc.vector.tensor_tensor(ebt_lo[:, :], ebt[:, :], ebt_hi[:, :].bitcast(F32), ALU.subtract)\
              .then_inc(expert_lo_ready, 1)
            add_skip(1)

            def group(g, it, k):
                tables_next = there(g + UNROLL - k)
                if there(g - 2):
                    low_weights(g - 2)
                masked(g, it, k, 0, 0)
                if there(g - 2):
                    scale(g - 2, k - 2, 0)
                    scale(g - 2, k - 2, 1)
                    mix(g - 2, k - 2, 0)
                if tables_next and k == 1:
                    reduce_phases(it + 1, 0, HB, *steady, steps=(0, 1))
                if there(g + 1):
                    split(g + 1, k + 1)
                masked(g, it, k, 0, 1)
                if tables_next and k == 2:
                    make_tables(it + 1, 0, HB, *steady)
                if there(g - 1):
                    add_logits(g - 1)
                    dve.wait_ge(token_ready, g)
                if there(g - 2):
                    mix(g - 2, k - 2, 1)
                if there(g - 1):
                    softmax(g - 1)
                if tables_next and k == 1:
                    reduce_phases(it + 1, 0, HB, *steady, steps=(2, 3, 4))
                masked(g, it, k, 1, 0)
                if there(g + 2):
                    add_skip(g + 2)
                masked(g, it, k, 1, 1)

            run(dve, group, G)
            low_weights(G - 2)
            scale(G - 2, UNROLL - 2, 0)
            scale(G - 2, UNROLL - 2, 1)
            add_logits(G - 1)
            dve.wait_ge(token_ready, G)
            softmax(G - 1)
            mix(G - 2, UNROLL - 2, 0)
            low_weights(G - 1)
            mix(G - 2, UNROLL - 2, 1)
            for half in range(2):
                scale(G - 1, UNROLL - 1, half)
            for half in range(2):
                mix(G - 1, UNROLL - 1, half)
            last_residual()

        @block.tensor
        def _(pe):
            def filters_of(g, it, k):
                if isinstance(g, int) and g == 0:
                    pe.wait_ge(head_dve, 10)
                else:
                    pe.wait_ge(tab_dve, 10 * (it + k // UNROLL) + 10)
                    pe.wait_ge(k_copied, g)
                if not (isinstance(g, int) and g < 4):
                    pe.wait_ge(scaled, 2 * g - 6)
                for j in range(2):
                    hb = 2 * (k % UNROLL) + j
                    ins = nc.tensor.matmul(filter_p[:, j * NI:(j + 1) * NI], tab_w[:, hb, :], tab_v[:, hb, :],
                                           start=True, stop=True)
                ins.then_inc(filter_mm, 1)

            def convolve(g, it, k, j, half):
                first = HALF * half
                if isinstance(g, int) and g == 0 and j == 0:
                    pe.wait_ge(first_lo_ready, half + 1)
                elif half == 0:
                    pe.wait_ge(toe_lo_ready, 2 * g + j + 1)
                if half == 0 and j == 0:
                    pe.wait_ge(u_lo_ready, g + 1)
                if not (isinstance(g, int) and g == 0):
                    pe.wait_ge(z_half, 4 * g + 2 * j + half - 3)
                parts = ((toe_hi[j], u_hi[k % 2]), (toe_hi[j], u_lo[k % 2]), (toe_lo[j], u_hi[k % 2]))
                work = [(0, 0)] + [(d, p) for d in range(1, first + HALF) for p in range(3)] + [(0, 1), (0, 2)]
                for n, (d, p) in enumerate(work):
                    tile, u = parts[p]
                    lo, hi = max(first, d), first + HALF
                    ins = nc.tensor.matmul(y[j][:, lo:hi, :], tile[:, d * P:(d + 1) * P],
                                           u[:, lo - d:hi - d, j, :], start=(n == 0), stop=(n == len(work) - 1))
                ins.then_inc(conv_half, 1)

            def logits(g, k):
                pe.wait_ge(z_half, 4 * g + 4)
                if not (isinstance(g, int) and g == 0):
                    pe.wait_ge(halves_ready, g)
                    pe.wait_ge(weight_t_ready, g)
                for q in range(NC // 2):
                    for odd in range(2):
                        ins = nc.tensor.matmul(logit_p[odd * E:(odd + 1) * E, :], rwt[:, 2 * q + odd, :],
                                               zs[k % 4][:, 2 * q + odd, :, :], start=(q == 0),
                                               stop=(q == NC // 2 - 1))
                ins.then_inc(logits_mm, 1)

            def tokens(g):
                pe.wait_ge(logit_t_ready, g + 1)
                for j in range(2):
                    ins = nc.tensor.transpose(token_p[:, j * P:(j + 1) * P], logit_t[:, j * B:(j + 1) * B],
                                              ident[:, :])
                ins.then_inc(token_mm, 1)

            def weights(g):
                pe.wait_ge(weights_ready, g + 1)
                if not (isinstance(g, int) and g == 0):
                    pe.wait_ge(weight_t_ready, g)
                for j in range(2):
                    ins = nc.tensor.transpose(weight_p[:, j * B:(j + 1) * B],
                                              weight2[:, j, :, :].rearrange("p t e -> p (t e)"), ident[:, :])
                ins.then_inc(weight_mm, 1)

            def weight_sums(g):
                if not (isinstance(g, int) and g == 0):
                    pe.wait_ge(scaled, 2 * g)
                pe.wait_ge(k_copied, min(g + 4, G) if isinstance(g, int) else g + 4)
                pe.wait_ge(weight_t_ready, g + 1)
                nc.tensor.matmul(wsum_p, ones[:, :], weight_t[:, :], start=True, stop=True)\
                  .then_inc(wsum_mm, 1)

            def bias(g, half):
                if isinstance(g, int) and g == 0 and half == 0:
                    pe.wait_ge(expert_lo_ready, 1)
                if isinstance(g, int) and g >= G - 2 and half == 1:
                    pe.wait_ge(z_half, 4 * G)
                elif not (isinstance(g, int) and g == 0 and half == 0):
                    pe.wait_ge(mixed, 2 * g + half)
                for q in range(2):
                    for odd in range(2):
                        cols = bass.ts(4 * half + 2 * q + odd, P)
                        nc.tensor.matmul(bias_in(g, half)[:, odd, q, :], ebt_hi[:, cols], weight_t[:, :],
                                         start=True, stop=False)
                        ins = nc.tensor.matmul(bias_in(g, half)[:, odd, q, :], ebt_lo[:, cols], weight_t[:, :],
                                               start=False, stop=True)
                ins.then_inc(bias_mm, 1)

            filters_of(0, 0, 0)
            filters_of(1, 0, 1)
            pe.wait_ge(consts_loaded, 96)
            pe.wait_ge(zeros_made, 2)

            def group(g, it, k):
                convolve(g, it, k, 0, 0)
                if there(g - 2):
                    weight_sums(g - 2)
                if there(g - 1):
                    logits(g - 1, k - 1)
                if there(g - 2):
                    bias(g - 2, 0)
                convolve(g, it, k, 0, 1)
                if there(g - 1):
                    tokens(g - 1)
                if there(g - 2):
                    bias(g - 2, 1)
                convolve(g, it, k, 1, 0)
                if there(g + 2):
                    filters_of(g + 2, it, k + 2)
                convolve(g, it, k, 1, 1)
                if there(g - 1):
                    weights(g - 1)

            run(pe, group, G)
            weight_sums(G - 2)
            logits(G - 1, UNROLL - 1)
            tokens(G - 1)
            bias(G - 2, 0)
            bias(G - 2, 1)
            weights(G - 1)
            weight_sums(G - 1)
            bias(G - 1, 0)
            bias(G - 1, 1)


def kernel(x, itok_B_78_3631, L0_cond_log_dt, L0_cond_C, L0_cond_log_A_real, L0_cond_A_imag, L0_cond_D,
           L0_ffn_router_weight, L0_ffn_router_bias, L0_ffn_expert_bias):
    import concourse.bacc as bacc
    from concourse.bass_utils import run_bass_kernel_spmd

    f32 = np.float32
    x, length = np.asarray(x), np.asarray(itok_B_78_3631)
    log_dt, c_in = np.asarray(L0_cond_log_dt), np.asarray(L0_cond_C)
    log_a, a_im, d = np.asarray(L0_cond_log_A_real), np.asarray(L0_cond_A_imag), np.asarray(L0_cond_D)
    rw, rb, eb = (np.asarray(a) for a in (L0_ffn_router_weight, L0_ffn_router_bias, L0_ffn_expert_bias))

    def twice(a):
        return np.concatenate([a.T, a.T], axis=0)

    modes = np.stack([np.broadcast_to(log_dt, (P, H)), twice(log_a), twice(a_im), twice(c_in[:, :, 0]),
                      twice(c_in[:, :, 1])], axis=1)
    steps = np.concatenate([np.arange(NI), NI * np.arange(NA), NI * np.arange(NA)])
    cosine_first = np.repeat([0.25, 0.0], N)[:, None]
    offsets = np.concatenate([np.broadcast_to(cosine_first, (P, NI + NA)),
                              np.broadcast_to(0.25 - cosine_first, (P, NA))], axis=1)
    by_group = x.reshape(B, G, 2, NC, P).transpose(1, 4, 3, 2, 0)
    sent = {
        "x": by_group.reshape(G, P, 2 * L),
        "x_rev": by_group[:, ::-1].reshape(G, P, 2 * L),
        "lens": np.broadcast_to(length, (P, B)),
        "modes": modes,
        "d_skip": d.reshape(1, H),
        "router": rw.reshape(E, NC, P).transpose(2, 1, 0),
        "router_bias": np.concatenate([rb, np.zeros(E, rb.dtype)]).reshape(P, 1),
        "expert_bias": np.concatenate([eb, eb], axis=0),
        "steps": np.broadcast_to(steps, (P, NJ)).astype(f32),
        "offsets": offsets.astype(f32),
        "l_index": (np.arange(P)[:, None] + P * np.arange(NC)[None, :]).astype(f32),
        "identity": np.eye(P, dtype=f32),
    }
    sent = {name: np.ascontiguousarray(a) for name, a in sent.items()}

    nc = bacc.Bacc("TRN2", target_bir_lowering=False, num_devices=1)
    aps = {name: nc.dram_tensor(f"in_{name}", a.shape, mybir.dt.from_np(a.dtype), kind="ExternalInput").ap()
           for name, a in sent.items()}
    out = nc.dram_tensor("out_dram", (G, P, 2 * L), F32, kind="ExternalOutput").ap()
    build(nc, out=out, **aps)
    result = run_bass_kernel_spmd(nc, [{f"in_{name}": a for name, a in sent.items()}], core_ids=[0])
    got = result.results[0]["out_dram"]
    return got.reshape(G, P, NC, 2, B).transpose(4, 0, 3, 2, 1).reshape(B, H, L)
```
